# Optimizing a Trainium2 kernel written in Bass

```python
import numpy as np
import jax
import jax.numpy as jnp

def _softmax(x, axis=-1):
    return jax.nn.softmax(x, axis=axis)

def _gelu(x):
    return jax.nn.gelu(x, approximate=True)

def _silu(x):
    return jax.nn.silu(x)

def _sigmoid(x):
    return jax.nn.sigmoid(x)

def _layernorm(x, axis=-1, eps=1e-05):
    m = jnp.mean(x, axis=axis, keepdims=True)
    v = jnp.var(x, axis=axis, keepdims=True)
    return (x - m) / jnp.sqrt(v + eps)

def _scatter_add(tgt, idx, src, axis=0):
    return tgt.at[idx].add(src)

def _segment_sum(src, seg, n):
    return jax.ops.segment_sum(src, seg, n)
kernel_name = 'mk_adj_ffn_d2_adj_r2_6f4992'

def setup_inputs(seed: int=0):
    np.random.seed(seed)
    _w = jnp.asarray

    def _rec_inputs():
        import jax
        import jax.numpy as jnp
        _gk = jax.random.key(seed)
        x = -0.0005207 + 1.001 * jax.random.normal(jax.random.fold_in(_gk, 1), (4096, 128), jnp.float32)
        _w = (1.0 + jnp.arange(4096, dtype=jnp.float32)) ** (-0.5)
        _w = _w / _w.mean()
        _pij = jnp.clip(0.00390625 * _w[:, None] * _w[None, :], 0.0, 1.0)
        _a = jax.random.uniform(jax.random.fold_in(_gk, 2), (4096, 4096)) < _pij
        _a = jnp.logical_or(_a, jnp.eye(4096, dtype=bool))
        _af = _a.astype(jnp.float32)
        adj = _af
        return (x, adj)
    x, adj = _rec_inputs()

    def _L0_gnn_setup():
        import jax, jax.numpy as jnp
        import numpy as np
        N = 4096
        E = 4096
        C = 128
        ALPHA = 0.1
        BETA = 0.5
        key = jax.random.key(seed)
        k1, k2, k3 = jax.random.split(key, 3)
        x_0 = jax.random.normal(k1, (N, C), dtype=jnp.float32)
        mask = (jax.random.uniform(k2, (N, E)) < 0.004).astype(jnp.float32)
        idx = jnp.arange(N)
        incidence_1 = mask.at[idx, idx].set(1.0)
        W = jax.random.normal(k3, (C, C), dtype=jnp.float32) / jnp.sqrt(C)
        return {'x_0': x_0, 'incidence_1': incidence_1, 'W': W}
    _L0_gnn_all = _L0_gnn_setup()
    _L0_gnn_in = {k: v for k, v in _L0_gnn_all.items() if k in ('W',)}
    del _L0_gnn_all

    def _L0_ffn_setup():
        import jax, jax.numpy as jnp
        import numpy as np
        D_MODEL = 128
        EXPERT_DIM = 256
        NUM_EXPERTS = 8
        TOP_K = 2
        SEQ_LEN = 1024
        BATCH = 2
        key = jax.random.key(seed)
        ks = jax.random.split(key, 8)
        s = 0.02
        x = jax.random.normal(ks[0], (SEQ_LEN, BATCH, D_MODEL), dtype=jnp.float32)
        Wg = jax.random.normal(ks[1], (D_MODEL, NUM_EXPERTS), dtype=jnp.float32) * s
        bg = jax.random.normal(ks[2], (NUM_EXPERTS,), dtype=jnp.float32) * s
        bias = jnp.zeros((NUM_EXPERTS,), dtype=jnp.float32)
        W1 = jax.random.normal(ks[3], (NUM_EXPERTS, D_MODEL, EXPERT_DIM), dtype=jnp.float32) * s
        b1 = jax.random.normal(ks[4], (NUM_EXPERTS, EXPERT_DIM), dtype=jnp.float32) * s
        W2 = jax.random.normal(ks[5], (NUM_EXPERTS, EXPERT_DIM, D_MODEL), dtype=jnp.float32) * s
        b2 = jax.random.normal(ks[6], (NUM_EXPERTS, D_MODEL), dtype=jnp.float32) * s
        return {'x': x, 'Wg': Wg, 'bg': bg, 'bias': bias, 'W1': W1, 'b1': b1, 'W2': W2, 'b2': b2}
    _L0_ffn_all = _L0_ffn_setup()
    _L0_ffn_in = {k: v for k, v in _L0_ffn_all.items() if k in ('Wg', 'bg', 'bias', 'W1', 'b1', 'W2', 'b2')}
    del _L0_ffn_all

    def _L1_gnn_setup():
        import jax, jax.numpy as jnp
        import numpy as np
        N = 3072
        HID = 128
        T = 350
        DENSITY = 0.05
        key = jax.random.key(seed)
        k1, k2, k3, k4, k5, k6 = jax.random.split(key, 6)
        h = jax.random.normal(k1, (N, HID), dtype=jnp.float32)
        a = jax.random.uniform(k2, (N, N), dtype=jnp.float32)
        mask = jax.random.uniform(k3, (N, N)) < DENSITY
        adj = jnp.where(mask, a, 0.0)
        simlar = jax.random.normal(k4, (N, N), dtype=jnp.float32)
        s = 1.0 / np.sqrt(HID)
        W_proj = jax.random.uniform(k5, (HID, HID), minval=-s, maxval=s, dtype=jnp.float32)
        b_proj = jnp.zeros((HID,), dtype=jnp.float32)
        W_gcn = jax.random.uniform(k6, (HID, HID), minval=-s, maxval=s, dtype=jnp.float32)
        b_gcn = jnp.zeros((HID,), dtype=jnp.float32)
        return {'h': h, 'adj': adj, 'simlar': simlar, 'W_proj': W_proj, 'b_proj': b_proj, 'W_gcn': W_gcn, 'b_gcn': b_gcn}
    _L1_gnn_all = _L1_gnn_setup()
    _L1_gnn_in = {k: v for k, v in _L1_gnn_all.items() if k in ('W_proj', 'b_proj', 'W_gcn', 'b_gcn')}
    del _L1_gnn_all

    def _L1_ffn_setup():
        import jax, jax.numpy as jnp
        import numpy as np
        D_IN, D_HID, D_OUT = (128, 256, 128)
        N_EXPERTS, TOP_K = (64, 2)
        B, S = (8, 2048)
        key = jax.random.key(seed)
        ks = jax.random.split(key, 8)
        scale_in = 1.0 / np.sqrt(D_IN)
        scale_hid = 1.0 / np.sqrt(D_HID)
        return {'x': jax.random.normal(ks[0], (B, S, D_IN), dtype=jnp.float32), 'Wr': jax.random.uniform(ks[1], (D_IN, N_EXPERTS), jnp.float32, -scale_in, scale_in), 'br': jax.random.uniform(ks[2], (N_EXPERTS,), jnp.float32, -scale_in, scale_in), 'W1': jax.random.uniform(ks[3], (N_EXPERTS, D_IN, D_HID), jnp.float32, -scale_in, scale_in), 'b1': jax.random.uniform(ks[4], (N_EXPERTS, D_HID), jnp.float32, -scale_in, scale_in), 'W2': jax.random.uniform(ks[5], (N_EXPERTS, D_HID, D_OUT), jnp.float32, -scale_hid, scale_hid), 'b2': jax.random.uniform(ks[6], (N_EXPERTS, D_OUT), jnp.float32, -scale_hid, scale_hid)}
    _L1_ffn_all = _L1_ffn_setup()
    _L1_ffn_in = {k: v for k, v in _L1_ffn_all.items() if k in ('Wr', 'br', 'W1', 'b1', 'W2', 'b2')}
    del _L1_ffn_all
    return {'x': x, 'adj': adj, 'L0_gnn_W': _L0_gnn_in['W'], 'L0_ffn_Wg': _L0_ffn_in['Wg'], 'L0_ffn_bg': _L0_ffn_in['bg'], 'L0_ffn_bias': _L0_ffn_in['bias'], 'L0_ffn_W1': _L0_ffn_in['W1'], 'L0_ffn_b1': _L0_ffn_in['b1'], 'L0_ffn_W2': _L0_ffn_in['W2'], 'L0_ffn_b2': _L0_ffn_in['b2'], 'L1_gnn_W_proj': _L1_gnn_in['W_proj'], 'L1_gnn_b_proj': _L1_gnn_in['b_proj'], 'L1_gnn_W_gcn': _L1_gnn_in['W_gcn'], 'L1_gnn_b_gcn': _L1_gnn_in['b_gcn'], 'L1_ffn_Wr': _L1_ffn_in['Wr'], 'L1_ffn_br': _L1_ffn_in['br'], 'L1_ffn_W1': _L1_ffn_in['W1'], 'L1_ffn_b1': _L1_ffn_in['b1'], 'L1_ffn_W2': _L1_ffn_in['W2'], 'L1_ffn_b2': _L1_ffn_in['b2']}

def reference(x, adj, L0_gnn_W, L0_ffn_Wg, L0_ffn_bg, L0_ffn_bias, L0_ffn_W1, L0_ffn_b1, L0_ffn_W2, L0_ffn_b2, L1_gnn_W_proj, L1_gnn_b_proj, L1_gnn_W_gcn, L1_gnn_b_gcn, L1_ffn_Wr, L1_ffn_br, L1_ffn_W1, L1_ffn_b1, L1_ffn_W2, L1_ffn_b2):
    import jax
    import jax.numpy as jnp

    def _L0_gnn_ref(x_0, incidence_1, W):
        import jax, jax.numpy as jnp
        import numpy as np
        N = 4096
        E = 4096
        C = 128
        ALPHA = 0.1
        BETA = 0.5
        m_0_1 = incidence_1.T @ x_0
        node_degree = jnp.sum(incidence_1, axis=1)
        edge_degree = node_degree @ incidence_1 / jnp.sum(incidence_1, axis=0)
        m_1_0 = incidence_1 @ (m_0_1 / jnp.sqrt(edge_degree)[:, None]) / jnp.sqrt(node_degree)[:, None]
        x_combined = (1.0 - ALPHA) * m_1_0 + ALPHA * x_0
        return (1.0 - BETA) * x_combined + BETA * (x_combined @ W.T)

    def _L0_ffn_ref(x, Wg, bg, bias, W1, b1, W2, b2):
        import jax, jax.numpy as jnp
        import numpy as np
        D_MODEL = 128
        EXPERT_DIM = 256
        NUM_EXPERTS = 8
        TOP_K = 2
        SEQ_LEN = 1024
        BATCH = 2
        x_flat = x.reshape(-1, D_MODEL)
        gate_logits = x_flat @ Wg + bg + bias
        topk_vals, topk_idx = jax.lax.top_k(gate_logits, TOP_K)
        topk_w = jax.nn.softmax(topk_vals, axis=-1)
        combine = (jax.nn.one_hot(topk_idx, NUM_EXPERTS, dtype=x.dtype) * topk_w[..., None]).sum(axis=1)
        h = jax.nn.relu(jnp.einsum('td,edh->teh', x_flat, W1) + b1)
        y = jnp.einsum('teh,ehd->ted', h, W2) + b2
        out = jnp.einsum('ted,te->td', y, combine)
        return out.reshape(x.shape)

    def _L1_gnn_ref(h, adj, simlar, W_proj, b_proj, W_gcn, b_gcn):
        import jax, jax.numpy as jnp
        import numpy as np
        N = 3072
        HID = 128
        T = 350
        DENSITY = 0.05
        sim = jnp.tanh(adj * simlar)
        filt = sim * (adj > 0).astype(sim.dtype)
        vals, idx = jax.lax.top_k(filt, T)
        nnz = jnp.sum(filt != 0, axis=1)
        keep = jnp.arange(T)[None, :] < nnz[:, None]
        rows = jnp.arange(filt.shape[0])[:, None]
        new_adj = jnp.zeros_like(filt).at[rows, idx].set(jnp.where(keep, vals, 0.0))
        h2 = jnp.tanh(h @ W_proj + b_proj)
        feat = jax.nn.relu(new_adj @ (h2 @ W_gcn) + b_gcn)
        return feat

    def _L1_ffn_ref(x, Wr, br, W1, b1, W2, b2):
        import jax, jax.numpy as jnp
        import numpy as np
        D_IN, D_HID, D_OUT = (128, 256, 128)
        N_EXPERTS, TOP_K = (64, 2)
        B, S = (8, 2048)
        Bx, Sx, D = x.shape
        xf = x.reshape(-1, D)
        T = xf.shape[0]
        E = Wr.shape[1]
        logits = xf @ Wr + br
        topk_logits, topk_idx = jax.lax.top_k(logits, TOP_K)
        gates = jax.nn.softmax(topk_logits, axis=1)
        combine = jnp.zeros((T, E), xf.dtype).at[jnp.arange(T)[:, None], topk_idx].add(gates)
        out = jnp.zeros((T, W2.shape[-1]), xf.dtype)
        for e in range(E):
            h = jax.nn.relu(xf @ W1[e] + b1[e])
            y = h @ W2[e] + b2[e]
            out = out + combine[:, e:e + 1] * y
        return out.reshape(Bx, Sx, -1)
    x = x + _L0_gnn_ref(_layernorm(x, axis=-1), adj, L0_gnn_W)
    x = x + _L0_ffn_ref(_layernorm(x, axis=-1)[None], L0_ffn_Wg, L0_ffn_bg, L0_ffn_bias, L0_ffn_W1, L0_ffn_b1, L0_ffn_W2, L0_ffn_b2)[0]
    x = x + _L1_gnn_ref(_layernorm(x, axis=-1), adj, adj, L1_gnn_W_proj, L1_gnn_b_proj, L1_gnn_W_gcn, L1_gnn_b_gcn)
    x = x + _L1_ffn_ref(_layernorm(x, axis=-1)[None], L1_ffn_Wr, L1_ffn_br, L1_ffn_W1, L1_ffn_b1, L1_ffn_W2, L1_ffn_b2)[0]
    return x

_drawn_inputs = setup_inputs


def setup_inputs(seed=0):
    import zlib

    import numpy as np

    out = dict(_drawn_inputs(seed))
    spreads = {'L0_ffn_bias': (0.0, 0.339), 'L1_gnn_b_proj': (0.0, 0.1), 'L1_gnn_b_gcn': (0.0, 0.1)}
    factors = {'L0_ffn_bg': 24.338,
     'L0_ffn_b1': 8.0,
     'L0_ffn_b2': 3.686,
     'L1_ffn_b1': 7.422,
     'L1_ffn_b2': 4.274}
    for name, (base, spread) in spreads.items():
        noise = np.random.default_rng([zlib.crc32(name.encode()), seed]).standard_normal(out[name].shape)
        drawn = base * np.exp(spread * noise) if base else spread * noise
        out[name] = jnp.asarray(drawn.astype(out[name].dtype))
    for name, factor in factors.items():
        out[name] = (out[name] * factor).astype(out[name].dtype)
    return out
```

```python
from contextlib import ExitStack

import concourse.bass as bass
from concourse import mybir

N, D, HID = 4096, 128, 256
P = 128
NT = N // P
NK = N // 256
E0, E1 = 8, 64
KEEP = 350
EPS = 1e-5
GRP = 2
CH = 3
NCH = -(-2 * NK // CH)
MW = D + 2
RING = 4
ORDER = [("T", 0), ("T", 1), ("C", 0), ("C", 1), ("C", 2), ("T", 2), ("C", 3), ("C", 4), ("C", 5), ("T", 3)] + \
        [("C", c) for c in range(6, NCH)]


def slot_tiles(n_experts):
    need = 2 * N // P + n_experts - 1
    return -(-need // RING) * RING


def program(nc, x, adj, w_gnn0, wg, bg, bias0, w1_0, b1_0, w2_0, b2_0,
            w_proj, b_proj, w_gcn, b_gcn, wr, br, w1_1, b1_1, w2_1, b2_1, out):
    f32, f16, bf16 = mybir.dt.float32, mybir.dt.float16, mybir.dt.bfloat16
    f8, u16, i32, u32 = mybir.dt.float8e4, mybir.dt.uint16, mybir.dt.int32, mybir.dt.uint32
    ALU, ACT, AX = mybir.AluOpType, mybir.ActivationFunctionType, mybir.AxisListType
    ctx = ExitStack()
    with ctx:
        def sb(name, shape, dt):
            return ctx.enter_context(nc.sbuf_tensor(name, shape, dt))

        def sem(name):
            return ctx.enter_context(nc.semaphore(name))

        slots_dram = nc.dram_tensor("slots", (slot_tiles(E1) * P, D), f32, kind="Internal").ap()
        results_dram = nc.dram_tensor("results", (slot_tiles(E1) * P, D), f32, kind="Internal").ap()

        adjT = sb("adjT", [P, NT, NK * P], u16)
        big1 = sb("big1", [P, 2 * NK * MW], f32)
        big2 = sb("big2", [P, N], f32)
        big3 = sb("big3", [P, N], f32)
        X = sb("X", [P, NT, D], f32)
        adj_words = adjT[:, :, :].rearrange("p t w -> p (t w)").bitcast(f32)
        msum = big1[:, :].rearrange("p (e c) -> p e c", c=MW)
        comb = big1[:, 0:N].rearrange("p (t c) -> p t c", c=D)
        gath = [big2[:, :].rearrange("p (t c) -> p t c", c=D), comb]
        stage = big2[:, :].rearrange("p (s c) -> p s c", s=4)
        XN = big2[:, :].rearrange("p (t c) -> p t c", c=D)
        nat = big3[:, :].bitcast(f8).rearrange("p (u j e) -> p u j e", u=2, j=GRP)
        Z = big3[:, :].bitcast(f16).rearrange("p (e c) -> p e c", c=2 * D)
        block_words = big2[:, 0:NK * P].bitcast(u16).rearrange("p (u w) -> p u w", u=2)
        block8 = big2[:, 0:NK * P].bitcast(f8).rearrange("p (u k n b) -> p u k n b", u=2, k=NK, b=2)
        cut_rows, cut_count = big2[:, :], big3[:, :]
        cut_nat = big1[:, 0:N // 4].bitcast(f8)
        w1s = big3[:, 0:RING * HID].rearrange("p (s c) -> p s c", s=RING)
        w2s = big3[:, 1024:1024 + RING * HID].rearrange("p (s h c) -> p s h c", s=RING, h=2)
        xss = big3[:, 2048:2048 + RING * D].rearrange("p (s c) -> p s c", s=RING)
        yss = big3[:, 2560:2560 + RING * D].rearrange("p (s c) -> p s c", s=RING)
        xTs = big3[:, 3072:3072 + 2 * D].rearrange("p (s c) -> p s c", s=2)
        hTs = big3[:, 3328:3328 + 2 * HID].rearrange("p (s h c) -> p s h c", s=2, h=2)

        def fours(big):
            v = big[:, 0:6 * 4 * D].rearrange("p (a u c) -> p a u c", a=3, u=2)
            return v[:, 0], v[:, 1], v[:, 2]

        ident = sb("ident", [P, P], f32)
        identb = sb("identb", [P, P], bf16)
        before = sb("before", [P, P], bf16)
        ones = sb("ones", [P, P], bf16)
        iotaE = sb("iotaE", [P, E1], f32)
        step128 = sb("step128", [P, NT], f32)
        iotaP = sb("iotaP", [P, 1], f32)
        zero1 = sb("zero1", [P, 1], f32)
        wmix = sb("wmix", [P, D], f32)
        wproj_s = sb("wproj_s", [P, D], f32)
        wgcn_s = sb("wgcn_s", [P, D], f32)
        wr0_s = sb("wr0_s", [P, E0], f32)
        wr1_s = sb("wr1_s", [P, E1], f32)
        rb0 = sb("rb0", [P, 2, E0], f32)
        rb1 = sb("rb1", [P, E1], f32)
        bproj_s = sb("bproj_s", [P, 1], f32)
        bgcn_s = sb("bgcn_s", [P, D], f32)
        b1T0 = sb("b1T0", [P, 2, E0], f32)
        b1T1 = sb("b1T1", [P, 2, E1], f32)
        xr = sb("xr", [P, 2, GRP, 2, MW], f16)
        xf = sb("xf", [P, GRP, D], f32)
        dpart = sb("dpart", [P, 2, GRP, 4], f32)
        deg = sb("deg", [P, NT], f32)
        rsd = sb("rsd", [P, NT], f32)
        redge = sb("redge", [P, NT], f32)
        small = sb("small", [P, 4, NT], f32)
        gsmall = sb("gsmall", [P, 2, NT], f32)
        stats = sb("stats", [P, NT, 6], f32)
        mean = sb("mean", [P, NT], f32)
        rstd = sb("rstd", [P, NT], f32)
        rstd01 = sb("rstd01", [P, NT], f32)
        l4 = sb("l4", [P, 4, E1], f32)
        top = sb("top", [P, 4, 8], f32)
        topi = sb("topi", [P, 4, 8], u32)
        val12 = sb("val12", [P, NT, 2], f32)
        idx12 = sb("idx12", [P, NT, 2], f32)
        gate = sb("gate", [P, 2, NT], f32)
        posf = sb("posf", [P, 2, NT], f32)
        pos = sb("pos", [P, 2, NT], i32)
        expt = sb("expt", [P, 5, E1], f32)
        eidc = sb("eidc", [P, 1], f32)
        eid = sb("eid", [1, P], i32)
        tanh1 = sb("tanh1", [P, 1], f32)
        ysum = big2[:, 3072:3328].rearrange("p (u c) -> p u c", u=2)
        ylow = big2[:, 3328:3584].rearrange("p (u c) -> p u c", u=2)
        degmax = sb("degmax", [P, NT], f32)
        cuti = sb("cuti", [1, NT], i32)
        wnat = adj_words[:, 0:D]
        b1n1 = adj_words[0:E1, 128:128 + HID]
        b1n0 = adj_words[0:E0, 384:384 + HID]
        iotas = adj_words[:, 1024:1024 + E1 + NT + 1].bitcast(i32)

        PS = ctx.enter_context(nc.psum_tensor("PS", [P, 8, 512], f32))
        psT = [PS[:, b, :].bitcast(bf16).rearrange("p (k n) -> p k n", n=P) for b in range(2)]
        psM = [PS[:, 2 + b, 0:CH * MW].rearrange("p (e c) -> p e c", c=MW) for b in range(6)]
        psY = [PS[:, b, 0:2 * D] for b in range(2)]
        psC = [PS[:, 2 + b, :] for b in range(2)]
        psR = [PS[:, 4 + b, :] for b in range(2)]
        psH2 = [PS[:, 6 + b, :] for b in range(2)]
        psX = [PS[:, b, 0:P] for b in range(2)]
        psH = [PS[:, 2 + b, 0:2 * P].rearrange("p (h n) -> p h n", h=2) for b in range(2)]
        psO = [PS[:, 4 + b, 0:D] for b in range(2)]
        banks = PS[:, :, :].rearrange("p b c -> p (b c)")

        x_loaded, weights_loaded, constants_ready = sem("x_loaded"), sem("weights_loaded"), sem("constants_ready")
        setup_T, setup_used = sem("setup_T"), sem("setup_used")
        arrived = [sem(f"quarter{s}_arrived") for s in range(4)]
        cast_done = sem("quarter_cast")
        words_T, words_free = sem("words_transposed"), sem("words_bank_free")
        chunk_done, chunk_free = sem("chunk_multiplied"), sem("chunk_bank_free")
        xr_ready = sem("group_tokens_ready")
        root_in, root_out = sem("root_input"), sem("root_output")
        z_ready = sem("operand_ready")
        blk_ready, y_done, y_low, y_free = sem("block_ready"), sem("product_done"), sem("product_low_copied"), sem("product_bank_free")
        four_ready, four_T, four_Tc, four_mm, four_free = (sem(n) for n in (
            "four_ready", "four_transposed", "four_T_copied", "four_multiplied", "four_used"))
        xn_copied, h2_done, h2_act = sem("normalized_copied"), sem("h2_multiplied"), sem("h2_active")
        cnt_ready, cnt_done = sem("choices_ready"), sem("counts_done")
        eid_col, eid_row, eid_ready, pos_ready = (sem(n) for n in ("expert_column", "expert_row", "experts_ready", "slots_ready"))
        gate_in, gate_exp = sem("gate_difference"), sem("gate_exp")
        prefilled, b2_loaded = sem("slots_prefilled"), sem("b2_loaded")
        scattered = sem("scattered")
        loaded = [sem(f"ring{s}_loaded") for s in range(RING)]
        xT_done, xT_copied, h_done, h_act, o_done, o_copied = (sem(n) for n in (
            "slot_transposed", "slot_T_copied", "hidden_done", "hidden_active", "result_done", "result_copied"))
        stored = [sem(f"ring{s}_stored") for s in range(RING)]
        gathered = [sem(f"gathered{b}") for b in range(NT // 4)]
        combined, out_written = sem("combined"), sem("output_written")
        deg_ready, cut_flag, cut_loaded, cut_masked, cut_T, cut_put = (sem(n) for n in (
            "degrees_ready", "cut_flags", "cut_rows_loaded", "cut_masked", "cut_transposed", "cut_put"))
        tanh_ready = sem("tanh1_ready")
        dve_steps, pool_steps = sem("dve_steps"), sem("pool_steps")

        wait_regs = {}

        def wait_apart(eng, *waits):
            regs = wait_regs.setdefault(eng.engine, [])
            while len(regs) < len(waits):
                regs.append(eng.alloc_register(f"awaited{len(regs)}"))
            for (_, n), reg in zip(waits, regs):
                eng.reg_mov(reg, n)
            eng.wait_ge(constants_ready, 1)
            for (s, _), reg in zip(waits, regs):
                eng.wait_ge(s, reg)

        class Steps:

            def __init__(self, eng, s):
                self.eng, self.sem, self.n = eng, s, 0

            def __call__(self, ins, alone=False):
                self.n = self.n + 1
                ins.then_inc(self.sem, 1)
                if alone:
                    wait_apart(self.eng, (self.sem, self.n))
                else:
                    self.eng.wait_ge(self.sem, self.n)

        T0, T1 = slot_tiles(E0), slot_tiles(E1)
        layers = [
            dict(n=0, E=E0, wr=wr0_s, w1=w1_0, w2=w2_0, b2=b2_0, b1T=b1T0, tiles=T0, jb=0, tmp=big1[:, :],
                 b2s=big1[:, 3072:3072 + E0 * D], four=big3, q=1),
            dict(n=1, E=E1, wr=wr1_s, w1=w1_1, w2=w2_1, b2=b2_1, b1T=b1T1, tiles=T1, jb=T0, tmp=adj_words,
                 b2s=adj_words[:, 20480:20480 + E1 * D], four=big3, q=3),
        ]
        for L in layers:
            w = L["E"] * NT
            L["part"] = [L["tmp"][:, i * w:(i + 1) * w] for i in range(8)]
            L["oh"] = [L["part"][0].bitcast(bf16)[:, k * w:(k + 1) * w] for k in (0, 1)]
            L["both"] = L["part"][1].bitcast(bf16)[:, 0:w]
        mix = dict(q=0, four=big3)
        proj = dict(q=2, four=big2)
        NF = NT // 4

        def ring_rounds(eng, tiles, body):
            for s in range(RING):
                body(0, s, s)
            with eng.Fori(1, tiles // RING - 1) as i:
                for s in range(RING):
                    body(i, s, i * RING + s)
            for s in range(RING):
                body(tiles // RING - 1, s, tiles - RING + s)

        def fill_ahead(eng, fill, use):
            fill(0, 0)
            with eng.Fori(0, NF // 2 - 1) as h:
                fill(h * 2 + 1, 1)
                use(h * 2, 0)
                fill(h * 2 + 2, 0)
                use(h * 2 + 1, 1)
            fill(NF - 1, 1)
            use(NF - 2, 0)
            use(NF - 1, 1)

        block = ctx.enter_context(nc.Block())

        @block.sync
        def _(sp):
            for s in range(RING):
                sp.sem_inc(stored[s], 16)
            sp.dma_start(X[:, :, :], x.rearrange("(t p) c -> p t c", p=P)).then_inc(x_loaded, 16)
            for s in range(4):
                sp.dma_start(stage[:, s, :], adj[0:P, s * 1024:(s + 1) * 1024]).then_inc(arrived[s], 16)
            row = lambda a, n: a.rearrange("(a n) -> a n", a=1).to_broadcast((P, n))
            for dst, src in (
                    (wnat, w_gnn0), (b1n1, b1_1), (b1n0, b1_0), (wproj_s[:, :], w_proj), (wgcn_s[:, :], w_gcn),
                    (wr0_s[:, :], wg), (wr1_s[:, :], wr), (rb0[:, 0, :], row(bg, E0)), (rb0[:, 1, :], row(bias0, E0)),
                    (rb1[:, :], row(br, E1)), (bproj_s[:, :], b_proj.rearrange("(n a) -> n a", a=1)),
                    (bgcn_s[:, :], row(b_gcn, D))):
                sp.dma_start(dst, src).then_inc(weights_loaded, 16)

            with sp.Fori(0, NT - 1) as t:
                for s in range(4):
                    sp.wait_ge(cast_done, t * 4 + s + 1)
                    sp.dma_start(stage[:, s, :], adj[bass.ds((t + 1) * P, P), s * 1024:(s + 1) * 1024]) \
                      .then_inc(arrived[s], 16)

            for r in range(T1 // NT):
                sp.dma_start(slots_dram[r * N:(r + 1) * N, :].rearrange("(t p) c -> p t c", p=P),
                             X[:, :, :]).then_inc(prefilled, 16)

            def expert_traffic(L):
                sp.wait_ge(four_free, 2 + NF * (L["q"] + 1))
                if L["n"]:
                    sp.wait_ge(y_free, 2 + 2 * NT)
                sp.dma_start(L["b2s"], L["b2"].rearrange("e (a c) -> a (e c)", a=1).to_broadcast((P, L["E"] * D))) \
                  .then_inc(b2_loaded, 16)
                sp.wait_ge(eid_ready, 1 + L["n"])
                sp.wait_ge(scattered, 16 * 2 * NT * (1 + L["n"]))

                def load(s, j):
                    e = sp.value_load(eid[0:1, bass.ds(j, 1)], min_val=0, max_val=L["E"] - 1)
                    sp.dma_start(w1s[:, s:s + 1, :], L["w1"][bass.ds(e, 1), :, :].rearrange("e p c -> p e c")) \
                      .then_inc(loaded[s], 16)
                    sp.dma_start(w2s[:, s, :, :], L["w2"][bass.ds(e, 1), :, :].rearrange("e (h p) c -> p (e h) c", p=P)) \
                      .then_inc(loaded[s], 16)
                    sp.dma_start(xss[:, s, :], slots_dram[bass.ds(j * P, P), :]).then_inc(loaded[s], 16)

                def store(s, j):
                    sp.wait_ge(o_copied, j + (L["jb"] + 3))
                    sp.dma_start(results_dram[bass.ds(j * P, P), :], yss[:, s, :]).then_inc(stored[s], 16)

                for s in range(RING):
                    load(s, s)
                with sp.Fori(0, L["tiles"] // RING - 1) as i:
                    for s in range(RING):
                        wait_apart(sp, (o_done, i * RING + (s + L["jb"] + 3)))
                        load(s, i * RING + (s + RING))
                        store(s, i * RING + s)
                for s in range(RING):
                    store(s, L["tiles"] - RING + s)

            expert_traffic(layers[0])

            sp.wait_ge(cut_flag, 1)
            sp.wait_ge(combined, NF)
            with sp.Fori(0, NT) as t:
                n = sp.value_load(cuti[0:1, bass.ds(t, 1)], min_val=0, max_val=N)
                with sp.If(n > KEEP):
                    sp.dma_start(cut_rows, adj[bass.ds(t * P, P), :]).then_inc(cut_loaded, 16)
                with sp.Else():
                    sp.sem_inc(cut_loaded, 16)
                wait_apart(sp, (cut_put, t + 1))

            expert_traffic(layers[1])
            for b in range(NF):
                sp.wait_ge(combined, NF + b + 1)
                sp.dma_start(out[b * 4 * P:(b + 1) * 4 * P, :].rearrange("(t p) c -> p t c", p=P),
                             X[:, 4 * b:4 * b + 4, :]).then_inc(out_written, 16)
            sp.wait_ge(out_written, 16 * NF)

        @block.gpsimd
        def _(pool):
            step = Steps(pool, pool_steps)
            for m in (ident, identb, before):
                step(pool.memset(m[:, :], 0.0))
            step(pool.memset(ones[:, :], 1.0))
            step(pool.memset(zero1[:, :], 0.0))
            for m in (ident, identb):
                step(pool.affine_select(out=m[:, :], in_=m[:, :], compare_op=ALU.not_equal, fill=1.0, base=0,
                                        pattern=[[-1, P]], channel_multiplier=1))
            step(pool.affine_select(out=before[:, :], in_=before[:, :], compare_op=ALU.is_ge, fill=1.0, base=0,
                                    pattern=[[-1, P]], channel_multiplier=1))
            step(pool.iota(iotas[:, 0:E1], [[1, E1]], base=0, channel_multiplier=0))
            step(pool.iota(iotas[:, E1:E1 + NT], [[P, NT]], base=0, channel_multiplier=0))
            step(pool.iota(iotas[:, E1 + NT:E1 + NT + 1], [[1, 1]], base=0, channel_multiplier=1))
            step(pool.tensor_copy(iotaE[:, :], iotas[:, 0:E1]))
            step(pool.tensor_copy(step128[:, :], iotas[:, E1:E1 + NT]))
            pool.tensor_copy(iotaP[:, :], iotas[:, E1 + NT:E1 + NT + 1]).then_inc(constants_ready, 1)

            pool.wait_ge(deg_ready, 1)
            step(pool.partition_all_reduce(degmax[:, :], deg[:, :], P, bass.bass_isa.ReduceOp.max))
            pool.tensor_copy(cuti[0:1, :], degmax[0:1, :]).then_inc(cut_flag, 1)

            def exchange(L):
                pool.wait_ge(pos_ready, 1 + L["n"])
                pool.wait_ge(xn_copied, NF * (1 + L["n"]))
                pool.wait_ge(prefilled, 16 * (T1 // NT))
                for t in range(NT):
                    for k in range(2):
                        pool.indirect_dma_start(
                            out=slots_dram, out_offset=bass.IndirectOffsetOnAxis(ap=pos[:, k, t:t + 1], axis=0),
                            in_=XN[:, t, :], in_offset=None).then_inc(scattered, 16)
                pool.wait_ge(scattered, 16 * 2 * NT * (1 + L["n"]))
                for s in range(RING):
                    pool.wait_ge(stored[s], 16 + 16 * ((L["tiles"] + L["jb"]) // RING))
                for b in range(NF):
                    for t in range(4 * b, 4 * b + 4):
                        for k in range(2):
                            pool.indirect_dma_start(
                                out=gath[k][:, t, :], out_offset=None, in_=results_dram[0:L["tiles"] * P, :],
                                in_offset=bass.IndirectOffsetOnAxis(ap=pos[:, k, t:t + 1], axis=0)) \
                                .then_inc(gathered[b], 16)

            exchange(layers[0])
            exchange(layers[1])

        @block.scalar
        def _(act):
            def cast(gg, u):
                for j in range(GRP):
                    for s in range(4):
                        free = [(chunk_done, gg * (2 * NCH) + (u + 1) * NCH)] if j + s == 0 else []
                        wait_apart(act, *free, (arrived[s], gg * 64 + 16 * (2 * u + j + 1)))
                        nc.scalar.activation(nat[:, u, j, s * 1024:(s + 1) * 1024], stage[:, s, :], ACT.Copy,
                                             accum_out=dpart[:, u, j, s:s + 1], saturate=False).then_inc(cast_done, 1)

            roots = [0]

            def root():
                roots[0] += 1
                act.wait_ge(root_in, roots[0])
                nc.scalar.activation(small[:, 1, :], small[:, 0, :], ACT.Sqrt).then_inc(root_out, 1)

            cast(0, 0)
            root()
            cast(0, 1)
            with act.Fori(1, NT // (2 * GRP)) as gg:
                cast(gg, 0)
                cast(gg, 1)
            root()
            root()

            def low_parts(r, scale):
                with act.Fori(0, NT // 2) as h:
                    for u in range(2):
                        act.wait_ge(y_done, h * 2 + (r * NT + u + 1))
                        act.wait_ge(y_free, h * 2 + (r * NT + u + 1))
                        nc.scalar.activation(ylow[:, u, :], psY[u][:, D:2 * D], ACT.Copy,
                                             scale=scale(h * 2 + u)).then_inc(y_low, 1)

            def transposes_out(p, keep=False, hidden=False):
                four, fourT, h2T = fours(p["four"])
                with act.Fori(0, NF // 2) as h:
                    for u in range(2):
                        i = h * 2 + u
                        act.wait_ge(four_T, i + (NF * p["q"] + 1))
                        act.wait_ge(four_mm, i + (NF * p["q"] + 1))
                        nc.scalar.activation(fourT[:, u, :], psC[u], ACT.Copy).then_inc(four_Tc, 1)
                        if keep:
                            nc.scalar.activation(XN[:, bass.ds(i * 4, 4), :].rearrange("p t c -> p (t c)"),
                                                 four[:, u, :], ACT.Copy).then_inc(xn_copied, 1)
                        if hidden:
                            act.wait_ge(h2_done, i + 1)
                            nc.scalar.activation(h2T[:, u, :], psH2[u], ACT.Tanh, bias=bproj_s[:, :]) \
                              .then_inc(h2_act, 1)

            def experts(L):
                act.wait_ge(gate_in, 1 + L["n"])
                nc.scalar.activation(gsmall[:, 1, :], gsmall[:, 0, :], ACT.Exp).then_inc(gate_exp, 1)
                act.wait_ge(eid_ready, 1 + L["n"])

                def hidden(i, s, j):
                    e = act.value_load(eid[0:1, bass.ds(j, 1)], min_val=0, max_val=L["E"] - 1)
                    act.wait_ge(h_done, j + (L["jb"] + 3))
                    act.wait_ge(o_done, j + (L["jb"] + 1))
                    for h in range(2):
                        last = nc.scalar.activation(hTs[:, s % 2, h, :], psH[s % 2][:, h, :], ACT.Relu,
                                                    bias=L["b1T"][:, h, bass.ds(e, 1)])
                    last.then_inc(h_act, 1)

                with act.Fori(0, L["tiles"] // RING) as i:
                    for s in range(RING):
                        hidden(i, s, i * RING + s)

            low_parts(0, lambda t: rsd[:, bass.ds(t, 1)])
            transposes_out(mix)
            root()
            transposes_out(layers[0], keep=True)
            experts(layers[0])
            root()
            act.wait_ge(constants_ready, 1)
            nc.scalar.activation(tanh1[:, :], ones[:, 0:1], ACT.Tanh).then_inc(tanh_ready, 1)
            transposes_out(proj, hidden=True)
            low_parts(1, lambda t: 1.0)
            root()
            transposes_out(layers[1], keep=True)
            experts(layers[1])

        @block.vector
        def _(dve):
            v = nc.vector
            step = Steps(dve, dve_steps)
            dve.sem_inc(chunk_free, NCH)
            dve.sem_inc(words_free, 2)
            dve.sem_inc(y_free, 2)
            dve.sem_inc(four_free, 2)
            dve.sem_inc(o_copied, 2)
            roots = [0]

            def inverse_root(dst, src_op, scale):
                roots[0] += 1
                src_op(small[:, 0, :]).then_inc(root_in, 1)
                dve.wait_ge(root_in, roots[0])
                dve.wait_ge(root_out, roots[0])
                step(v.reciprocal(small[:, 2, :], small[:, 1, :]))
                step(v.tensor_tensor(small[:, 2, :], small[:, 2, :], small[:, 0, :], ALU.mult))
                step(v.tensor_tensor(small[:, 2, :], small[:, 2, :], small[:, 1, :], ALU.add))
                step(v.reciprocal(small[:, 3, :], small[:, 2, :]))
                step(v.tensor_scalar(dst[:, :], small[:, 3, :], 2.0 * scale, None, ALU.mult))

            def norm_stats():
                a, b, c = small[:, 1, :], small[:, 2, :], small[:, 3, :]
                step(v.tensor_tensor(a, stats[:, :, 1], stats[:, :, 4], ALU.add))
                step(v.tensor_scalar(mean[:, :], a, 0.5, None, ALU.mult))
                step(v.tensor_tensor(b, stats[:, :, 1], stats[:, :, 4], ALU.subtract))
                step(v.tensor_tensor(b, b, b, ALU.mult))
                step(v.tensor_tensor(c, stats[:, :, 2], stats[:, :, 5], ALU.add))
                step(v.scalar_tensor_tensor(c, b, D / 4.0, c, ALU.mult, ALU.add))
                inverse_root(rstd, lambda o: v.tensor_scalar(o, c, 1.0 / D, EPS, ALU.mult, ALU.add), 1.0)

            step(v.memset(big1[:, :], 0.0))
            step(v.memset(xr[:, :, :, 0, D + 1:MW], 1.0))
            step(v.memset(xr[:, :, :, 1, D + 1:MW], 0.0))
            dve.wait_ge(x_loaded, 16)
            with dve.Fori(0, NF) as i:
                for j in range(4):
                    last = v.bn_stats(stats[:, bass.ds(i * 4 + j, 1), :].rearrange("p t c -> p (t c)"),
                                      X[:, bass.ds(i * 4 + j, 1), :].rearrange("p t c -> p (t c)"))
                last.then_inc(dve_steps, 1)
            step.n += NF
            dve.wait_ge(dve_steps, step.n)
            norm_stats()
            step(v.tensor_scalar(rstd01[:, :], rstd[:, :], 0.1, None, ALU.mult))
            dve.wait_ge(setup_T, 1)
            dve.wait_ge(constants_ready, 1)
            step(v.scalar_tensor_tensor(wmix[:, :], PS[:, 2, 0:D], 1.0, ident[:, :], ALU.mult, ALU.add))
            step(v.tensor_scalar(wmix[:, :], wmix[:, :], 0.5, None, ALU.mult))
            step(v.tensor_copy(b1T1[:, :, :], PS[:, 3, 0:2 * E1].rearrange("p (h e) -> p h e", h=2)))
            step(v.tensor_tensor(rb0[:, 0, :], rb0[:, 0, :], rb0[:, 1, :], ALU.add))
            v.tensor_copy(b1T0[:, :, :], PS[:, 4, 0:2 * E0].rearrange("p (h e) -> p h e", h=2)).then_inc(setup_used, 1)
            dve.wait_ge(setup_used, 1)

            def group(gg, u, chain):
                g = gg * 2 + u

                n = [0]

                def chained(ins):
                    n[0] += 1
                    ins.then_inc(dve_steps, 1)
                    wait_apart(dve, (dve_steps, chain + n[0]))

                for j in range(GRP):
                    chained(v.tensor_scalar(xf[:, j, :], X[:, bass.ds(g * GRP + j, 1), :].rearrange("p t c -> p (t c)"),
                                            mean[:, bass.ds(g * GRP + j, 1)], rstd[:, bass.ds(g * GRP + j, 1)],
                                            ALU.subtract, ALU.mult))
                wait_apart(dve, (chunk_done, g * NCH + NCH), (cast_done, g * (4 * GRP) + 4 * GRP))
                chained(v.tensor_copy(xr[:, u, :, 0, 0:D], xf[:, :, :]))
                v.tensor_tensor(xr[:, u, :, 1, 0:D], xf[:, :, :], xr[:, u, :, 0, 0:D], ALU.subtract)
                chained(v.reduce_sum(deg[:, bass.ds(g * GRP, GRP)], dpart[:, u, :, :], AX.X))
                chained(v.tensor_copy(xr[:, u, :, 0, D:D + 1].rearrange("p j c -> p (j c)"), deg[:, bass.ds(g * GRP, GRP)]))
                v.tensor_tensor(xr[:, u, :, 1, D:D + 1].rearrange("p j c -> p (j c)"), deg[:, bass.ds(g * GRP, GRP)],
                                xr[:, u, :, 0, D:D + 1].rearrange("p j c -> p (j c)"), ALU.subtract).then_inc(xr_ready, 1)

                def words(w):
                    wait_apart(dve, (words_T, g * 4 + w + 1))
                    v.tensor_copy(adjT[:, bass.ds(g * GRP + w // 2, 1), (w % 2) * 1024:(w % 2 + 1) * 1024]
                                  .rearrange("p t w -> p (t w)"),
                                  PS[:, w % 2, :].bitcast(u16)).then_inc(words_free, 1)

                def sums(c):
                    n = min(CH, 2 * NK - CH * c)
                    dve.wait_ge(chunk_done, g * NCH + (2 * NCH + c + 1))
                    dve.wait_ge(chunk_free, g * NCH + c + 1)
                    v.tensor_tensor(msum[:, CH * c:CH * c + n, :], psM[c % 6][:, 0:n, :],
                                    msum[:, CH * c:CH * c + n, :], ALU.add).then_inc(chunk_free, 1)

                for kind, i in ORDER:
                    (words if kind == "T" else sums)(i)

            base = step.n
            with dve.Fori(0, NT // (2 * GRP)) as gg:
                group(gg, 0, gg * 10 + base)
                group(gg, 1, gg * 10 + (base + 5))
            step.n = base + 10 * (NT // (2 * GRP))
            dve.wait_ge(chunk_free, NCH * (NT // GRP) + NCH)
            dve.wait_ge(xr_ready, NT // GRP)
            dve.sem_inc(deg_ready, 1)

            inverse_root(rsd, lambda o: v.tensor_copy(o, deg[:, :]), 0.9)
            step(v.reciprocal(small[:, 2, :], msum[:, :, D + 1]))
            inverse_root(redge, lambda o: v.tensor_tensor(o, msum[:, :, D], small[:, 2, :], ALU.mult), 1.0)
            for b in range(4):
                e = slice(8 * b, 8 * b + 8)
                step(v.tensor_tensor(msum[:, e, 0:D], msum[:, e, 0:D],
                                     redge[:, e].unsqueeze(2).to_broadcast((P, 8, D)), ALU.mult))
                step(v.tensor_copy(Z[:, e, 0:D], msum[:, e, 0:D]))
                v.tensor_tensor(Z[:, e, D:2 * D], msum[:, e, 0:D], Z[:, e, 0:D], ALU.subtract).then_inc(z_ready, 1)
            dve.wait_ge(z_ready, 4)

            def product(r, post, k):
                def copy_block(t, u):
                    v.tensor_copy(block_words[:, u, :], adjT[:, bass.ds(t, 1), :].rearrange("p t w -> p (t w)")) \
                     .then_inc(blk_ready, 1)

                def after(t, u, n):
                    dve.wait_ge(y_done, t + (r * NT + 1))
                    dve.wait_ge(y_low, t + (r * NT + 1))
                    post(t, u, n)

                base = step.n
                copy_block(0, 0)
                copy_block(1, 1)
                with dve.Fori(0, NT // 2 - 1) as h:
                    for u in range(2):
                        after(h * 2 + u, u, h * (2 * k) + (base + u * k))
                        copy_block(h * 2 + u + 2, u)
                for u in range(2):
                    after(NT - 2 + u, u, base + (NT - 2 + u) * k)
                step.n = base + NT * k

            def tile_of(a, t):
                return a[:, bass.ds(t, 1), :].rearrange("p t c -> p (t c)")

            def mixed(t, u, n):
                step.n = n
                v.scalar_tensor_tensor(ysum[:, u, :], psY[u][:, 0:D], rsd[:, bass.ds(t, 1)], ylow[:, u, :],
                                       ALU.mult, ALU.add).then_inc(y_free, 1)
                step(v.tensor_scalar(tile_of(comb, t), tile_of(X, t), mean[:, bass.ds(t, 1)], rstd01[:, bass.ds(t, 1)],
                                     ALU.subtract, ALU.mult))
                step(v.tensor_tensor(tile_of(comb, t), tile_of(comb, t), ysum[:, u, :], ALU.add))

            product(0, mixed, 2)

            def pass_fours(p, fill, use):
                def use_i(i, u):
                    dve.wait_ge(four_mm, i + (NF * p["q"] + 3))
                    use(i, u)

                fill_ahead(dve, fill, use_i)

            four, fourT, h2T = fours(big3)

            def fill_mix(i, u):
                v.tensor_copy(four[:, u, :], comb[:, bass.ds(i * 4, 4), :].rearrange("p t c -> p (t c)")) \
                 .then_inc(four_ready, 1)

            def use_mix(i, u):
                flat = X[:, bass.ds(i * 4, 4), :].rearrange("p t c -> p (t c)")
                v.tensor_tensor(flat, flat, psR[u], ALU.add).then_inc(four_free, 1)
                dve.wait_ge(four_free, i + 3)
                for j in range(4):
                    last = v.bn_stats(stats[:, bass.ds(i * 4 + j, 1), :].rearrange("p t c -> p (t c)"),
                                      tile_of(X, i * 4 + j))
                last.then_inc(dve_steps, 1)

            def fill_norm(p):
                four, _, _ = fours(p["four"])

                def fill(i, u):
                    for j in range(4):
                        last = v.tensor_scalar(four[:, u, j * D:(j + 1) * D], tile_of(X, i * 4 + j),
                                               mean[:, bass.ds(i * 4 + j, 1)], rstd[:, bass.ds(i * 4 + j, 1)],
                                               ALU.subtract, ALU.mult)
                    last.then_inc(four_ready, 1)
                return fill

            dve.wait_ge(prefilled, 16 * (T1 // NT))
            pass_fours(mix, fill_mix, use_mix)
            step.n += NF
            dve.wait_ge(dve_steps, step.n)
            norm_stats()

            def use_router(L):
                E = L["E"]
                bias = rb0[:, 0, :] if L["n"] == 0 else rb1[:, :]
                base = step.n

                def use(i, u):
                    step.n = i * 3 + base
                    dve.wait_ge(xn_copied, i + (NF * L["n"] + 1))
                    dve.wait_ge(dve_steps, step.n)
                    l3 = l4[:, :, 0:E]
                    v.tensor_tensor(l3, psR[u][:, 0:4 * E].rearrange("p (t e) -> p t e", t=4),
                                    bias.unsqueeze(1).to_broadcast((P, 4, E)), ALU.add).then_inc(four_free, 1)
                    wait_apart(dve, (four_free, i + (NF * L["q"] + 3)))
                    for j in range(4):
                        last = v.max(out=top[:, j, :], in_=l4[:, j, 0:E])
                    step(last, alone=True)
                    for j in range(4):
                        last = v.max_index(topi[:, j, :], top[:, j, :], l4[:, j, 0:E])
                    step(last, alone=True)
                    v.tensor_copy(val12[:, bass.ds(i * 4, 4), :], top[:, :, 0:2])
                    step(v.tensor_copy(idx12[:, bass.ds(i * 4, 4), :], topi[:, :, 0:2]))
                pass_fours(L, fill_norm(L), use)
                step.n = base + 3 * NF

            def route(L):
                E, n, part = L["E"], L["n"], L["part"]
                et = lambda a: a.rearrange("p (e t) -> p e t", t=NT)
                over_t = lambda a: a.unsqueeze(2).to_broadcast((P, E, NT))
                over_e = lambda a: a.unsqueeze(1).to_broadcast((P, E, NT))
                for k in range(2):
                    step(v.tensor_tensor(et(L["oh"][k]), over_t(iotaE[:, 0:E]), over_e(idx12[:, :, k]), ALU.is_equal))
                v.tensor_tensor(L["both"], L["oh"][0], L["oh"][1], ALU.add).then_inc(cnt_ready, 1)
                v.tensor_tensor(gsmall[:, 0, :], val12[:, :, 1], val12[:, :, 0], ALU.subtract).then_inc(gate_in, 1)
                dve.wait_ge(cnt_done, 1 + n)
                w = E * NT
                tot, rank = banks[:, 0:w], banks[:, 2048:2048 + w]
                run, excl, a, b = part[3], part[4], part[5], part[6]
                step(v.tensor_tensor_scan(run, zero1[:, :].to_broadcast((P, w)), tot, 0.0, ALU.add, ALU.add))
                step(v.tensor_tensor(excl, run, tot, ALU.subtract))
                count, tiles, upto, begin, shift = (expt[:, i, 0:E] for i in range(5))
                first = et(excl)[:, :, 0]
                step(v.tensor_tensor(count, et(run)[:, :, NT - 1], first, ALU.subtract))
                step(v.tensor_tensor(et(a), over_t(count), over_e(step128[:, :]), ALU.is_gt))
                step(v.reduce_sum(tiles, et(a), AX.X))
                step(v.tensor_tensor_scan(upto, zero1[:, :].to_broadcast((P, E)), tiles, 0.0, ALU.add, ALU.add))
                step(v.tensor_tensor(part[2][:, 0:E], upto, iotaP[:, :].to_broadcast((P, E)), ALU.is_le))
                step(v.reduce_sum(eidc[:, :], part[2][:, 0:E], AX.X))
                v.tensor_scalar(eidc[:, :], eidc[:, :], float(E - 1), None, ALU.min).then_inc(eid_col, 1)
                step(v.tensor_tensor(begin, upto, tiles, ALU.subtract))
                step(v.scalar_tensor_tensor(shift, begin, float(P), first, ALU.mult, ALU.subtract))
                dve.wait_ge(eid_row, 1 + n)
                v.tensor_copy(eid[:, :], PS[0:1, 0, 0:P]).then_inc(eid_ready, 1)
                step(v.tensor_tensor(et(a), et(excl), over_t(shift), ALU.add))
                step(v.tensor_tensor(a, a, rank, ALU.add))
                for k in range(2):
                    step(v.tensor_tensor(b, L["oh"][k], a, ALU.mult))
                    step(v.reduce_sum(posf[:, k, :], b.rearrange("p (e t) -> p t e", t=NT), AX.X))
                v.tensor_copy(pos[:, :, :], posf[:, :, :]).then_inc(pos_ready, 1)
                dve.wait_ge(gate_exp, 1 + n)
                step(v.tensor_scalar(gsmall[:, 0, :], gsmall[:, 1, :], 1.0, None, ALU.add))
                step(v.reciprocal(gate[:, 0, :], gsmall[:, 0, :]))
                step(v.tensor_tensor(gate[:, 1, :], gate[:, 0, :], gsmall[:, 1, :], ALU.mult))

            def expert_loop(L):
                jb = L["jb"]
                dve.wait_ge(b2_loaded, 16 * (1 + L["n"]))
                dve.wait_ge(eid_ready, 1 + L["n"])

                def turned(s, j):
                    dve.wait_ge(xT_done, j + (jb + 1))
                    dve.wait_ge(h_done, j + (jb + 1))
                    v.tensor_copy(xTs[:, s % 2, :], psX[s % 2]).then_inc(xT_copied, 1)

                def result(i, s, j):
                    e = dve.value_load(eid[0:1, bass.ds(j, 1)], min_val=0, max_val=L["E"] - 1)
                    dve.wait_ge(o_done, j + (jb + 3))
                    dve.wait_ge(stored[s], i * 16 + (16 * (jb // RING) + 16))
                    v.tensor_tensor(yss[:, s, :], psO[s % 2], L["b2s"][:, bass.ds(e * D, D)], ALU.add) \
                     .then_inc(o_copied, 1)

                turned(0, 0)

                def body(i, s, j):
                    if not isinstance(j, int) or j + 1 < L["tiles"]:
                        turned((s + 1) % RING, j + 1)
                    if not isinstance(j, int) or j > 0:
                        result(i if s else i - 1, (s - 1) % RING, j - 1)
                ring_rounds(dve, L["tiles"], body)
                result(L["tiles"] // RING - 1, RING - 1, L["tiles"] - 1)

            def combine(L):
                n = L["n"]
                for b in range(NF):
                    t = slice(4 * b, 4 * b + 4)
                    dve.wait_ge(gathered[b], 128 * (n + 1))
                    for k in range(2):
                        step(v.tensor_tensor(gath[k][:, t, :], gath[k][:, t, :],
                                             gate[:, k, t].unsqueeze(2).to_broadcast((P, 4, D)), ALU.mult))
                    step(v.tensor_tensor(gath[0][:, t, :], gath[0][:, t, :], gath[1][:, t, :], ALU.add))
                    v.tensor_tensor(X[:, t, :], X[:, t, :], gath[0][:, t, :], ALU.add).then_inc(combined, 1)
                    if n == 0:
                        dve.wait_ge(combined, b + 1)
                        for tt in range(4 * b, 4 * b + 4):
                            last = v.bn_stats(stats[:, tt, :], X[:, tt, :])
                        step(last)

            use_router(layers[0])
            route(layers[0])
            expert_loop(layers[0])
            combine(layers[0])
            norm_stats()

            dve.wait_ge(cut_flag, 1)
            with dve.Fori(0, NT) as t:
                n = dve.value_load(cuti[0:1, bass.ds(t, 1)], min_val=0, max_val=N)
                wait_apart(dve, (cut_loaded, t * 16 + 16))
                with dve.If(n > KEEP):
                    v.tensor_tensor_scan(cut_count, zero1[:, :].to_broadcast((P, N)), cut_rows, 0.0, ALU.add, ALU.add) \
                     .then_inc(dve_steps, 1)
                    wait_apart(dve, (dve_steps, t + (step.n + 1)))
                    v.scalar_tensor_tensor(cut_nat, cut_count, float(KEEP), cut_rows, ALU.is_le, ALU.mult, saturate=False) \
                     .then_inc(cut_masked, 1)
                with dve.Else():
                    dve.sem_inc(dve_steps, 1)
                    dve.sem_inc(cut_masked, 1)
                wait_apart(dve, (cut_T, t + 1))
                with dve.If(n > KEEP):
                    v.tensor_copy(adjT[:, bass.ds(t, 1), 0:1024].rearrange("p t w -> p (t w)"), PS[:, 0, :].bitcast(u16))
                    v.tensor_copy(adjT[:, bass.ds(t, 1), 1024:2048].rearrange("p t w -> p (t w)"), PS[:, 1, :].bitcast(u16)) \
                     .then_inc(cut_put, 1)
                with dve.Else():
                    dve.sem_inc(cut_put, 1)
            step.n += NT
            dve.wait_ge(cut_put, NT)

            dve.wait_ge(tanh_ready, 1)

            def use_proj(i, u):
                e4 = Z[:, bass.ds(i * 4, 4), 0:D]
                l4_ = Z[:, bass.ds(i * 4, 4), D:2 * D]
                src = psR[u].rearrange("p (e c) -> p e c", e=4)
                v.tensor_scalar(e4, src, tanh1[:, :], None, ALU.mult).then_inc(z_ready, 1)
                dve.wait_ge(z_ready, i + 5)
                v.scalar_tensor_tensor(l4_, src, tanh1[:, :], e4, ALU.mult, ALU.subtract).then_inc(four_free, 1)

            pass_fours(proj, fill_norm(proj), use_proj)
            dve.wait_ge(four_free, 2 + 3 * NF)

            def graph2(t, u, n):
                step.n = n
                v.tensor_tensor(ysum[:, u, :], psY[u][:, 0:D], ylow[:, u, :], ALU.add).then_inc(y_free, 1)
                dve.wait_ge(y_free, t + (NT + 3))
                step(v.tensor_tensor(ysum[:, u, :], ysum[:, u, :], bgcn_s[:, :], ALU.add))
                step(v.scalar_tensor_tensor(tile_of(X, t), ysum[:, u, :], 0.0, tile_of(X, t), ALU.max, ALU.add))
                step(v.bn_stats(stats[:, bass.ds(t, 1), :].rearrange("p t c -> p (t c)"), tile_of(X, t)))

            product(1, graph2, 3)
            norm_stats()
            use_router(layers[1])
            route(layers[1])
            expert_loop(layers[1])
            combine(layers[1])

        @block.tensor
        def _(pe):
            mm = nc.tensor.matmul
            pe.sem_inc(chunk_done, 2 * NCH)
            pe.sem_inc(four_mm, 2)
            pe.sem_inc(h_done, 2)
            pe.sem_inc(o_done, 2)
            pe.wait_ge(constants_ready, 1)
            pe.wait_ge(weights_loaded, 16 * 12)
            mm(PS[:, 2, 0:D], wnat, ident[:, :], start=True, stop=True)
            for h in range(2):
                mm(PS[:, 3, h * E1:(h + 1) * E1], b1n1[:, h * P:(h + 1) * P], ident[0:E1, 0:E1], start=True, stop=True)
            for h in range(2):
                last = mm(PS[:, 4, h * E0:(h + 1) * E0], b1n0[:, h * P:(h + 1) * P], ident[0:E0, 0:E0], start=True, stop=True)
            last.then_inc(setup_T, 1)
            pe.wait_ge(setup_used, 1)

            def turn_words(src, bank, half):
                words = src.bitcast(bf16)
                for k in range(8):
                    last = pe.transpose(psT[bank][:, k, :], words[:, (8 * half + k) * P:(8 * half + k + 1) * P], identb[:, :])
                return last

            def group(gg, u):
                g = gg * 2 + u
                pe.wait_ge(cast_done, g * (4 * GRP) + 4 * GRP)

                def words(w):
                    pe.wait_ge(words_free, g * 4 + w + 1)
                    turn_words(nat[:, u, w // 2, :], w % 2, w % 2).then_inc(words_T, 1)

                def sums(c):
                    n = min(CH, 2 * NK - CH * c)
                    wait_apart(pe, (chunk_free, g * NCH + (NCH + c - 5 if c >= 6 else c + 7 if c <= 4 else 6)),
                               (xr_ready, g + 1))
                    for e in range(n):
                        k, b = divmod(CH * c + e, 2)
                        for j in range(GRP):
                            a = nat[:, u, j, 256 * k + b:256 * (k + 1):2]
                            mm(psM[c % 6][:, e, :], a, xr[:, u, j, 0, :], start=(j == 0), stop=False)
                            last = mm(psM[c % 6][:, e, :], a, xr[:, u, j, 1, :], start=False, stop=(j == GRP - 1))
                    last.then_inc(chunk_done, 1)

                for kind, i in ORDER:
                    (words if kind == "T" else sums)(i)

            with pe.Fori(0, NT // (2 * GRP)) as gg:
                group(gg, 0)
                group(gg, 1)

            def product(r):
                with pe.Fori(0, NT // 2) as h:
                    for u in range(2):
                        t = h * 2 + u
                        wait_apart(pe, (blk_ready, t + (r * NT + 1)), (y_free, t + (r * NT + 1)))
                        for k in range(NK):
                            for b in range(2):
                                last = mm(psY[u], block8[:, u, k, :, b], Z[:, 2 * k + b, :],
                                          start=(k == 0 and b == 0), stop=(k == NK - 1 and b == 1))
                        last.then_inc(y_done, 1)

            def pass_fours(p, final):
                four, fourT, h2T = fours(p["four"])

                def turn(i, u):
                    pe.wait_ge(four_ready, i + (NF * p["q"] + 1))
                    for j in range(4):
                        last = pe.transpose(psC[u][:, j * P:(j + 1) * P], four[:, u, j * D:(j + 1) * D], ident[:, :])
                    last.then_inc(four_T, 1)

                def use(i, u):
                    pe.wait_ge(four_Tc, i + (NF * p["q"] + 1))
                    pe.wait_ge(four_free, i + (NF * p["q"] + 1))
                    final(i, u, fourT[:, u, :], h2T[:, u, :]).then_inc(four_mm, 1)

                fill_ahead(pe, turn, use)

            def by_tile(w, n):
                def final(i, u, fT, hT):
                    for j in range(4):
                        last = mm(psR[u][:, j * n:(j + 1) * n], fT[:, j * P:(j + 1) * P], w, start=True, stop=True)
                    return last
                return final

            def projected(i, u, fT, hT):
                mm(psH2[u], wproj_s[:, :], fT, start=True, stop=True).then_inc(h2_done, 1)
                pe.wait_ge(h2_act, i + 1)
                for k in range(2):
                    for b in range(2):
                        q = 2 * k + b
                        last = mm(psR[u][:, q * D:(q + 1) * D], hT[:, 256 * k + b:256 * (k + 1):2], wgcn_s[:, :],
                                  start=True, stop=True)
                return last

            def experts(L):
                E, jb = L["E"], L["jb"]
                w = E * NT
                pe.wait_ge(cnt_ready, 1 + L["n"])
                for m, at in ((ones, 0), (before, 2048)):
                    for c in range(0, w, 512):
                        n = min(512, w)
                        last = mm(banks[:, at + c:at + c + n], m[:, :], L["both"][:, c:c + n], start=True, stop=True)
                last.then_inc(cnt_done, 1)
                pe.wait_ge(eid_col, 1 + L["n"])
                mm(PS[0:1, 0, 0:P], eidc[:, :], ident[:, :], start=True, stop=True).then_inc(eid_row, 1)
                pe.wait_ge(pos_ready, 1 + L["n"])

                def turn(i, s, j):
                    pe.wait_ge(loaded[s], i * 48 + (48 * (jb // RING) + 48))
                    pe.transpose(psX[s % 2], xss[:, s, :], ident[:, :]).then_inc(xT_done, 1)

                def hidden(s, j):
                    pe.wait_ge(xT_copied, j + (jb + 1))
                    for h in range(2):
                        last = mm(psH[s % 2][:, h, :], w1s[:, s, h * P:(h + 1) * P], xTs[:, s % 2, :], start=True, stop=True)
                    last.then_inc(h_done, 1)

                def result(s, j):
                    pe.wait_ge(h_act, j + (jb + 1))
                    pe.wait_ge(o_copied, j + (jb + 1))
                    for h in range(2):
                        last = mm(psO[s % 2], hTs[:, s % 2, h, :], w2s[:, s, h, :], start=(h == 0), stop=(h == 1))
                    last.then_inc(o_done, 1)

                turn(0, 0, 0)

                def body(i, s, j):
                    if not isinstance(j, int) or j + 1 < L["tiles"]:
                        turn(i if s + 1 < RING else i + 1, (s + 1) % RING, j + 1)
                    hidden(s, j)
                    if not isinstance(j, int) or j > 0:
                        result((s - 1) % RING, j - 1)
                ring_rounds(pe, L["tiles"], body)
                result(RING - 1, L["tiles"] - 1)

            pe.wait_ge(z_ready, 4)
            product(0)
            pass_fours(mix, by_tile(wmix[:, :], D))
            pass_fours(layers[0], by_tile(wr0_s[:, :], E0))
            experts(layers[0])
            pe.wait_ge(cut_flag, 1)
            with pe.Fori(0, NT) as t:
                n = pe.value_load(cuti[0:1, bass.ds(t, 1)], min_val=0, max_val=N)
                pe.wait_ge(cut_masked, t + 1)
                with pe.If(n > KEEP):
                    turn_words(cut_nat, 0, 0)
                    turn_words(cut_nat, 1, 1).then_inc(cut_T, 1)
                with pe.Else():
                    pe.sem_inc(cut_T, 1)
            pass_fours(proj, projected)
            pe.wait_ge(z_ready, 4 + NF)
            product(1)
            pass_fours(layers[1], by_tile(wr1_s[:, :], E1))
            experts(layers[1])


_INS = ['x', 'adj', 'L0_gnn_W', 'L0_ffn_Wg', 'L0_ffn_bg', 'L0_ffn_bias', 'L0_ffn_W1', 'L0_ffn_b1', 'L0_ffn_W2',
        'L0_ffn_b2', 'L1_gnn_W_proj', 'L1_gnn_b_proj', 'L1_gnn_W_gcn', 'L1_gnn_b_gcn', 'L1_ffn_Wr', 'L1_ffn_br',
        'L1_ffn_W1', 'L1_ffn_b1', 'L1_ffn_W2', 'L1_ffn_b2']


def kernel(**inputs):
    import numpy as np
    import concourse.bacc as bacc
    from concourse.bass_utils import run_bass_kernel_spmd as run

    nc = bacc.Bacc("TRN2", target_bir_lowering=False, num_devices=1)
    arrays, args = {}, []
    for name in _INS:
        a = np.ascontiguousarray(inputs[name])
        arrays[f"in_{name}"] = a
        args.append(nc.dram_tensor(f"in_{name}", a.shape, mybir.dt.from_np(a.dtype), kind="ExternalInput").ap())
    args.append(nc.dram_tensor("out_0", (N, D), mybir.dt.float32, kind="ExternalOutput").ap())
    program(nc, *args)
    r = run(nc, [arrays], core_ids=[0])
    return r.results[0]["out_0"]
```

```python
from contextlib import ExitStack

import concourse.bass as bass
from concourse import mybir

N, D, HID = 4096, 128, 256
P = 128
NT = N // P
NK = N // 256
E0, E1 = 8, 64
KEEP = 350
EPS = 1e-5
GRP = 2
CH = 3
NCH = -(-2 * NK // CH)
MW = D + 2
RING = 8
XG = 4
WSCALE = 64.0
WW = 2 * HID
ORDER = [("T", 0), ("T", 1), ("C", 0), ("C", 1), ("C", 2), ("T", 2), ("C", 3), ("C", 4), ("C", 5), ("T", 3)] + \
        [("C", c) for c in range(6, NCH)]


def slot_tiles(n_experts):
    need = 2 * N // P + n_experts - 1
    return -(-need // RING) * RING


def program(nc, x, adj, w_gnn0, wg, bg, bias0, w1_0, b1_0, w2_0, b2_0,
            w_proj, b_proj, w_gcn, b_gcn, wr, br, w1_1, b1_1, w2_1, b2_1, out):
    f32, f16, bf16 = mybir.dt.float32, mybir.dt.float16, mybir.dt.bfloat16
    f8, u16, i32, u32 = mybir.dt.float8e4, mybir.dt.uint16, mybir.dt.int32, mybir.dt.uint32
    ALU, ACT, AX = mybir.AluOpType, mybir.ActivationFunctionType, mybir.AxisListType
    ctx = ExitStack()
    with ctx:
        def sb(name, shape, dt):
            return ctx.enter_context(nc.sbuf_tensor(name, shape, dt))

        def sem(name):
            return ctx.enter_context(nc.semaphore(name))

        slots_dram = nc.dram_tensor("slots", (slot_tiles(E1) * P, 2 * D), f16, kind="Internal").ap()
        results_dram = nc.dram_tensor("results", (slot_tiles(E1) * P, D), f32, kind="Internal").ap()
        packed_dram = [nc.dram_tensor(f"packed{n}", (E * P, 2 * WW), f16, kind="Internal").ap()
                       for n, E in ((0, E0), (1, E1))]

        adjT = sb("adjT", [P, NT, NK * P], u16)
        big1 = sb("big1", [P, 2 * NK * MW], f32)
        big2 = sb("big2", [P, N], f32)
        big3 = sb("big3", [P, N], f32)
        X = sb("X", [P, NT, D], f32)
        adj_words = adjT[:, :, :].rearrange("p t w -> p (t w)").bitcast(f32)
        msum = big1[:, :].rearrange("p (e c) -> p e c", c=MW)
        comb = big1[:, 0:N].rearrange("p (t c) -> p t c", c=D)
        gath = [big2[:, :].rearrange("p (t c) -> p t c", c=D), comb]
        stage = big2[:, :].rearrange("p (s c) -> p s c", s=4)
        XN = big2[:, :].bitcast(f16).rearrange("p (t c) -> p t c", c=2 * D)
        nat = big3[:, :].bitcast(f8).rearrange("p (u j e) -> p u j e", u=2, j=GRP)
        Z = big3[:, :].bitcast(f16).rearrange("p (e c) -> p e c", c=2 * D)
        block_words = big2[:, 0:NK * P].bitcast(u16).rearrange("p (u w) -> p u w", u=2)
        block8 = big2[:, 0:NK * P].bitcast(f8).rearrange("p (u k n b) -> p u k n b", u=2, k=NK, b=2)
        cut_rows, cut_count = big2[:, :], big3[:, :]
        cut_nat = big1[:, 0:N // 4].bitcast(f8)
        ws = big3[:, :].bitcast(f16).rearrange("p (s c) -> p s c", s=RING)
        w1s = ws.rearrange("p s (l c) -> p s l c", l=2)[:, :, :, 0:HID]
        w2s = ws.rearrange("p s (l c) -> p s l c", l=2)[:, :, :, HID:2 * HID]
        xss = big1[:, 0:2 * XG * D].bitcast(f16).rearrange("p (g s c) -> p g s c", g=2, s=XG)
        yss = big1[:, 1024:1024 + 2 * XG * D].rearrange("p (g s c) -> p g s c", g=2, s=XG)
        hTs = big1[:, 2048:2048 + 512].bitcast(f16).rearrange("p (s l h n) -> p s l h n", s=2, l=2, h=2)
        xTs = big1[:, 2560:2560 + 256].bitcast(f16).rearrange("p (s l n) -> p s l n", s=2, l=2)

        def fours(big):
            v = big[:, 0:6 * 4 * D].rearrange("p (a u c) -> p a u c", a=3, u=2)
            return v[:, 0], v[:, 1], v[:, 2]

        ident = sb("ident", [P, P], f32)
        identb = sb("identb", [P, P], bf16)
        identh = sb("identh", [P, P], f16)
        before = sb("before", [P, P], bf16)
        ones = sb("ones", [P, P], bf16)
        iotaE = sb("iotaE", [P, E1], f32)
        step128 = sb("step128", [P, NT], f32)
        iotaP = sb("iotaP", [P, 1], f32)
        zero1 = sb("zero1", [P, 1], f32)
        wmix = sb("wmix", [P, D], f32)
        wproj_s = sb("wproj_s", [P, D], f32)
        wgcn_s = sb("wgcn_s", [P, D], f32)
        wr0_s = sb("wr0_s", [P, E0], f32)
        wr1_s = sb("wr1_s", [P, E1], f32)
        rb0 = sb("rb0", [P, 2, E0], f32)
        rb1 = sb("rb1", [P, E1], f32)
        bproj_s = sb("bproj_s", [P, 1], f32)
        bgcn_s = sb("bgcn_s", [P, D], f32)
        b1T0 = sb("b1T0", [P, 2, E0], f32)
        b1T1 = sb("b1T1", [P, 2, E1], f32)
        xr = sb("xr", [P, 2, GRP, 2, MW], f16)
        xf = sb("xf", [P, GRP, D], f32)
        dpart = sb("dpart", [P, 2, GRP, 4], f32)
        deg = sb("deg", [P, NT], f32)
        rsd = sb("rsd", [P, NT], f32)
        redge = sb("redge", [P, NT], f32)
        small = sb("small", [P, 4, NT], f32)
        gsmall = sb("gsmall", [P, 2, NT], f32)
        stats = sb("stats", [P, NT, 6], f32)
        mean = sb("mean", [P, NT], f32)
        rstd = sb("rstd", [P, NT], f32)
        rstd01 = sb("rstd01", [P, NT], f32)
        l4 = sb("l4", [P, 4, E1], f32)
        top = sb("top", [P, 4, 8], f32)
        topi = sb("topi", [P, 4, 8], u32)
        val12 = sb("val12", [P, NT, 2], f32)
        idx12 = sb("idx12", [P, NT, 2], f32)
        gate = sb("gate", [P, 2, NT], f32)
        posf = sb("posf", [P, 2, NT], f32)
        pos = sb("pos", [P, 2, NT], i32)
        expt = sb("expt", [P, 5, E1], f32)
        eidc = sb("eidc", [P, 1], f32)
        eid = sb("eid", [1, P], i32)
        tanh1 = sb("tanh1", [P, 1], f32)
        ysum = big2[:, 3072:3328].rearrange("p (u c) -> p u c", u=2)
        ylow = big2[:, 3328:3584].rearrange("p (u c) -> p u c", u=2)
        degmax = sb("degmax", [P, NT], f32)
        cuti = sb("cuti", [1, NT], i32)
        wnat = adj_words[:, 0:D]
        b1n1 = adj_words[0:E1, 128:128 + HID]
        b1n0 = adj_words[0:E0, 384:384 + HID]
        iotas = adj_words[:, 1024:1024 + E1 + NT + 1].bitcast(i32)

        PS = ctx.enter_context(nc.psum_tensor("PS", [P, 8, 512], f32))
        psT = [PS[:, b, :].bitcast(bf16).rearrange("p (k n) -> p k n", n=P) for b in range(2)]
        psM = [PS[:, 2 + b, 0:CH * MW].rearrange("p (e c) -> p e c", c=MW) for b in range(6)]
        psY = [PS[:, b, 0:2 * D] for b in range(2)]
        psC = [PS[:, 2 + b, :] for b in range(2)]
        psR = [PS[:, 4 + b, :] for b in range(2)]
        psH2 = [PS[:, 6 + b, :] for b in range(2)]
        psX = [PS[:, b, 0:P].bitcast(f16).rearrange("p (l n) -> p l n", l=2) for b in range(2)]
        psH = [PS[:, 2 + b, 0:2 * P].rearrange("p (h n) -> p h n", h=2) for b in range(2)]
        psO = [PS[:, 4 + b, 0:D] for b in range(2)]
        banks = PS[:, :, :].rearrange("p b c -> p (b c)")

        x_loaded, weights_loaded, constants_ready = sem("x_loaded"), sem("weights_loaded"), sem("constants_ready")
        setup_T, setup_used = sem("setup_T"), sem("setup_used")
        arrived = [sem(f"quarter{s}_arrived") for s in range(4)]
        cast_done = sem("quarter_cast")
        words_T, words_free = sem("words_transposed"), sem("words_bank_free")
        chunk_done, chunk_free = sem("chunk_multiplied"), sem("chunk_bank_free")
        xr_ready = sem("group_tokens_ready")
        root_in, root_out = sem("root_input"), sem("root_output")
        z_ready = sem("operand_ready")
        blk_ready, y_done, y_low, y_free = sem("block_ready"), sem("product_done"), sem("product_low_copied"), sem("product_bank_free")
        four_ready, four_T, four_Tc, four_mm, four_free = (sem(n) for n in (
            "four_ready", "four_transposed", "four_T_copied", "four_multiplied", "four_used"))
        xn_copied, h2_done, h2_act = sem("normalized_copied"), sem("h2_multiplied"), sem("h2_active")
        cnt_ready, cnt_done = sem("choices_ready"), sem("counts_done")
        eid_col, eid_row, eid_ready, pos_ready = (sem(n) for n in ("expert_column", "expert_row", "experts_ready", "slots_ready"))
        gate_in, gate_exp = sem("gate_difference"), sem("gate_exp")
        prefilled, b2_loaded = sem("slots_prefilled"), sem("b2_loaded")
        scattered = sem("scattered")
        weights_in = [sem(f"ring{s}_loaded") for s in range(RING)]
        tokens_in = [sem(f"slot_group{s}_loaded") for s in range(2)]
        relu_done, split_low = sem("hidden_relu"), sem("hidden_low")
        pack_in = [[sem(f"experts{n}_{b}_loaded") for b in range(2 if n else 1)] for n in range(2)]
        pack_out = [[sem(f"experts{n}_{b}_stored") for b in range(2 if n else 1)] for n in range(2)]
        pack_done, pack_used = sem("expert_packed"), sem("pack_buffers_used")
        xn_ready = sem("normalized_split")
        xT_done, xT_copied, h_done, h_act, o_done, o_copied = (sem(n) for n in (
            "slot_transposed", "slot_T_copied", "hidden_done", "hidden_active", "result_done", "result_copied"))
        stored = [sem(f"slot_group{s}_stored") for s in range(2)]
        gathered = [sem(f"gathered{b}") for b in range(NT // 4)]
        combined, out_written = sem("combined"), sem("output_written")
        deg_ready, cut_flag, cut_loaded, cut_masked, cut_T, cut_put = (sem(n) for n in (
            "degrees_ready", "cut_flags", "cut_rows_loaded", "cut_masked", "cut_transposed", "cut_put"))
        tanh_ready = sem("tanh1_ready")
        dve_steps, pool_steps = sem("dve_steps"), sem("pool_steps")

        wait_regs = {}

        def wait_apart(eng, *waits):
            regs = wait_regs.setdefault(eng.engine, [])
            while len(regs) < len(waits):
                regs.append(eng.alloc_register(f"awaited{len(regs)}"))
            for (_, n), reg in zip(waits, regs):
                eng.reg_mov(reg, n)
            eng.wait_ge(constants_ready, 1)
            for (s, _), reg in zip(waits, regs):
                eng.wait_ge(s, reg)

        class Steps:

            def __init__(self, eng, s):
                self.eng, self.sem, self.n = eng, s, 0

            def __call__(self, ins, alone=False):
                self.n = self.n + 1
                ins.then_inc(self.sem, 1)
                if alone:
                    wait_apart(self.eng, (self.sem, self.n))
                else:
                    self.eng.wait_ge(self.sem, self.n)

        T0, T1 = slot_tiles(E0), slot_tiles(E1)
        layers = [
            dict(n=0, E=E0, wr=wr0_s, w1=w1_0, w2=w2_0, b2=b2_0, b1T=b1T0, tiles=T0, jb=0, tmp=big1[:, :],
                 b2s=big1[:, 3072:3072 + E0 * D], four=big3, q=1, pack=big2[:, 2048:3072], nb=1),
            dict(n=1, E=E1, wr=wr1_s, w1=w1_1, w2=w2_1, b2=b2_1, b1T=b1T1, tiles=T1, jb=T0, tmp=adj_words,
                 b2s=adj_words[:, 20480:20480 + E1 * D], four=big3, q=3, pack=big1[:, 0:2048], nb=2),
        ]
        for L in layers:
            w = L["E"] * NT
            L["part"] = [L["tmp"][:, i * w:(i + 1) * w] for i in range(8)]
            L["oh"] = [L["part"][0].bitcast(bf16)[:, k * w:(k + 1) * w] for k in (0, 1)]
            L["both"] = L["part"][1].bitcast(bf16)[:, 0:w]
            v_ = L["pack"].rearrange("p (b c) -> p b c", b=L["nb"])
            L["pack32"], L["pack16"] = v_[:, :, 0:WW], v_[:, :, WW:2 * WW]
        mix = dict(q=0, four=big3)
        proj = dict(q=2, four=big2)
        NF = NT // 4

        def ring_rounds(eng, tiles, body):
            for s in range(RING):
                body(0, s, s)
            with eng.Fori(1, tiles // RING - 1) as i:
                for s in range(RING):
                    body(i, s, i * RING + s)
            for s in range(RING):
                body(tiles // RING - 1, s, tiles - RING + s)

        def fill_ahead(eng, fill, use):
            fill(0, 0)
            with eng.Fori(0, NF // 2 - 1) as h:
                fill(h * 2 + 1, 1)
                use(h * 2, 0)
                fill(h * 2 + 2, 0)
                use(h * 2 + 1, 1)
            fill(NF - 1, 1)
            use(NF - 2, 0)
            use(NF - 1, 1)

        block = ctx.enter_context(nc.Block())

        @block.sync
        def _(sp):
            for g in range(2):
                sp.sem_inc(stored[g], 16)
            for L in layers:
                for b in range(L["nb"]):
                    sp.sem_inc(pack_out[L["n"]][b], 16)
            sp.dma_start(X[:, :, :], x.rearrange("(t p) c -> p t c", p=P)).then_inc(x_loaded, 16)
            for s in range(4):
                sp.dma_start(stage[:, s, :], adj[0:P, s * 1024:(s + 1) * 1024]).then_inc(arrived[s], 16)
            row = lambda a, n: a.rearrange("(a n) -> a n", a=1).to_broadcast((P, n))
            for dst, src in (
                    (wnat, w_gnn0), (b1n1, b1_1), (b1n0, b1_0), (wproj_s[:, :], w_proj), (wgcn_s[:, :], w_gcn),
                    (wr0_s[:, :], wg), (wr1_s[:, :], wr), (rb0[:, 0, :], row(bg, E0)), (rb0[:, 1, :], row(bias0, E0)),
                    (rb1[:, :], row(br, E1)), (bproj_s[:, :], b_proj.rearrange("(n a) -> n a", a=1)),
                    (bgcn_s[:, :], row(b_gcn, D))):
                sp.dma_start(dst, src).then_inc(weights_loaded, 16)

            with sp.Fori(0, NT - 1) as t:
                for s in range(4):
                    sp.wait_ge(cast_done, t * 4 + s + 1)
                    sp.dma_start(stage[:, s, :], adj[bass.ds((t + 1) * P, P), s * 1024:(s + 1) * 1024]) \
                      .then_inc(arrived[s], 16)

            sp.wait_ge(z_ready, 4)
            for r in range(T1 // NT):
                sp.dma_start(slots_dram[r * N:(r + 1) * N, :].rearrange("(t p) c -> p t c", p=P), Z).then_inc(prefilled, 16)

            def pack_traffic(L):
                nb, n = L["nb"], L["n"]
                base = n * E0

                def load(e, b):
                    sp.dma_start(L["pack32"][:, b:b + 1, 0:HID], L["w1"][bass.ds(e, 1), :, :].rearrange("e p c -> p e c")) \
                      .then_inc(pack_in[n][b], 16)
                    sp.dma_start(L["pack32"][:, b, HID:2 * HID].rearrange("p (h c) -> p h c", h=2),
                                 L["w2"][bass.ds(e, 1), :, :].rearrange("e (h p) c -> p (e h) c", p=P)) \
                      .then_inc(pack_in[n][b], 16)

                def store(e, b):
                    sp.wait_ge(pack_done, e + (base + 1))
                    sp.dma_start(packed_dram[n][bass.ds(e * P, P), :], L["pack16"][:, b, :].bitcast(f16)) \
                      .then_inc(pack_out[n][b], 16)

                for b in range(nb):
                    load(b, b)
                with sp.Fori(0, L["E"] // nb - 1) as i:
                    for b in range(nb):
                        store(i * nb + b, b)
                        load(i * nb + (b + nb), b)
                for b in range(nb):
                    store(L["E"] - nb + b, b)

            def expert_traffic(L):
                jb, n = L["jb"], L["n"]
                sp.wait_ge(four_free, 2 + NF * (L["q"] + 1))
                if n:
                    sp.wait_ge(y_free, 2 + 2 * NT)
                sp.dma_start(L["b2s"], L["b2"].rearrange("e (a c) -> a (e c)", a=1).to_broadcast((P, L["E"] * D))) \
                  .then_inc(b2_loaded, 16)
                for b in range(L["nb"]):
                    sp.wait_ge(pack_out[n][b], 16 + 16 * (L["E"] // L["nb"]))
                sp.wait_ge(eid_ready, 1 + n)

                def load(s, j):
                    e = sp.value_load(eid[0:1, bass.ds(j, 1)], min_val=0, max_val=L["E"] - 1)
                    sp.dma_start(ws[:, s, :], packed_dram[n][bass.ds(e * P, P), :]).then_inc(weights_in[s], 16)

                def load_tokens(g, j):
                    sp.dma_start(xss[:, g, :, :], slots_dram[bass.ds(j * P, XG * P), :].rearrange("(s p) c -> p s c", p=P)) \
                      .then_inc(tokens_in[g], 16)

                def store(g, j):
                    sp.wait_ge(o_copied, j + (jb + XG + 2))
                    sp.dma_start(results_dram[bass.ds(j * P, XG * P), :].rearrange("(s p) c -> p s c", p=P), yss[:, g, :, :]) \
                      .then_inc(stored[g], 16)

                for s in range(RING):
                    load(s, s)
                sp.wait_ge(pos_ready, 1 + n)
                sp.wait_ge(scattered, 16 * 2 * NT * (1 + n))
                for g in range(2):
                    load_tokens(g, g * XG)
                with sp.Fori(0, L["tiles"] // RING - 1) as i:
                    for s in range(RING):
                        wait_apart(sp, (o_done, i * RING + (s + jb + 3)))
                        load(s, i * RING + (s + RING))
                        if s % XG == XG - 1:
                            load_tokens(s // XG, i * RING + (RING + s - XG + 1))
                            store(s // XG, i * RING + (s - XG + 1))
                for g in range(2):
                    store(g, L["tiles"] - RING + g * XG)

            pack_traffic(layers[0])
            expert_traffic(layers[0])

            sp.wait_ge(cut_flag, 1)
            sp.wait_ge(combined, NF)
            with sp.Fori(0, NT) as t:
                n = sp.value_load(cuti[0:1, bass.ds(t, 1)], min_val=0, max_val=N)
                with sp.If(n > KEEP):
                    sp.dma_start(cut_rows, adj[bass.ds(t * P, P), :]).then_inc(cut_loaded, 16)
                with sp.Else():
                    sp.sem_inc(cut_loaded, 16)
                wait_apart(sp, (cut_put, t + 1))

            pack_traffic(layers[1])
            expert_traffic(layers[1])
            for b in range(NF):
                sp.wait_ge(combined, NF + b + 1)
                sp.dma_start(out[b * 4 * P:(b + 1) * 4 * P, :].rearrange("(t p) c -> p t c", p=P),
                             X[:, 4 * b:4 * b + 4, :]).then_inc(out_written, 16)
            sp.wait_ge(out_written, 16 * NF)

        @block.gpsimd
        def _(pool):
            step = Steps(pool, pool_steps)
            for m in (ident, identb, identh, before):
                step(pool.memset(m[:, :], 0.0))
            step(pool.memset(ones[:, :], 1.0))
            step(pool.memset(zero1[:, :], 0.0))
            for m in (ident, identb, identh):
                step(pool.affine_select(out=m[:, :], in_=m[:, :], compare_op=ALU.not_equal, fill=1.0, base=0,
                                        pattern=[[-1, P]], channel_multiplier=1))
            step(pool.affine_select(out=before[:, :], in_=before[:, :], compare_op=ALU.is_ge, fill=1.0, base=0,
                                    pattern=[[-1, P]], channel_multiplier=1))
            step(pool.iota(iotas[:, 0:E1], [[1, E1]], base=0, channel_multiplier=0))
            step(pool.iota(iotas[:, E1:E1 + NT], [[P, NT]], base=0, channel_multiplier=0))
            step(pool.iota(iotas[:, E1 + NT:E1 + NT + 1], [[1, 1]], base=0, channel_multiplier=1))
            step(pool.tensor_copy(iotaE[:, :], iotas[:, 0:E1]))
            step(pool.tensor_copy(step128[:, :], iotas[:, E1:E1 + NT]))
            pool.tensor_copy(iotaP[:, :], iotas[:, E1 + NT:E1 + NT + 1]).then_inc(constants_ready, 1)

            pool.wait_ge(deg_ready, 1)
            step(pool.partition_all_reduce(degmax[:, :], deg[:, :], P, bass.bass_isa.ReduceOp.max))
            pool.tensor_copy(cuti[0:1, :], degmax[0:1, :]).then_inc(cut_flag, 1)

            def pack(L):
                nb, n = L["nb"], L["n"]
                base = pool_steps_n[0]
                with pool.Fori(0, L["E"] // nb) as i:
                    for b in range(nb):
                        e = i * nb + b
                        high, low = (L["pack16"][:, b, :].bitcast(f16)[:, q * WW:(q + 1) * WW] for q in (0, 1))
                        wait_apart(pool, (pack_in[n][b], i * 32 + 32), (pack_out[n][b], i * 16 + 16))
                        pool.tensor_scalar(L["pack32"][:, b, :], L["pack32"][:, b, :], WSCALE, None, ALU.mult) \
                            .then_inc(pool_steps, 1)
                        wait_apart(pool, (pool_steps, e * 2 + (base + 1)))
                        pool.tensor_copy(high, L["pack32"][:, b, :]).then_inc(pool_steps, 1)
                        wait_apart(pool, (pool_steps, e * 2 + (base + 2)))
                        pool.tensor_tensor(low, L["pack32"][:, b, :], high, ALU.subtract).then_inc(pack_done, 1)
                pool_steps_n[0] = base + 2 * L["E"]

            def exchange(L):
                pool.wait_ge(pos_ready, 1 + L["n"])
                pool.wait_ge(xn_ready, NF * (1 + L["n"]))
                pool.wait_ge(prefilled, 16 * (T1 // NT))
                for t in range(NT):
                    for k in range(2):
                        pool.indirect_dma_start(
                            out=slots_dram, out_offset=bass.IndirectOffsetOnAxis(ap=pos[:, k, t:t + 1], axis=0),
                            in_=XN[:, t, :], in_offset=None).then_inc(scattered, 16)
                pool.wait_ge(scattered, 16 * 2 * NT * (1 + L["n"]))
                for g in range(2):
                    pool.wait_ge(stored[g], 16 + 16 * ((L["tiles"] + L["jb"]) // RING))
                for b in range(NF):
                    for t in range(4 * b, 4 * b + 4):
                        for k in range(2):
                            pool.indirect_dma_start(
                                out=gath[k][:, t, :], out_offset=None, in_=results_dram[0:L["tiles"] * P, :],
                                in_offset=bass.IndirectOffsetOnAxis(ap=pos[:, k, t:t + 1], axis=0)) \
                                .then_inc(gathered[b], 16)

            pool_steps_n = [step.n]
            pack(layers[0])
            exchange(layers[0])
            pack(layers[1])
            exchange(layers[1])

        @block.scalar
        def _(act):
            def cast(gg, u):
                for j in range(GRP):
                    for s in range(4):
                        free = [(chunk_done, gg * (2 * NCH) + (u + 1) * NCH)] if j + s == 0 else []
                        wait_apart(act, *free, (arrived[s], gg * 64 + 16 * (2 * u + j + 1)))
                        nc.scalar.activation(nat[:, u, j, s * 1024:(s + 1) * 1024], stage[:, s, :], ACT.Copy,
                                             accum_out=dpart[:, u, j, s:s + 1], saturate=False).then_inc(cast_done, 1)

            roots = [0]

            def root():
                roots[0] += 1
                act.wait_ge(root_in, roots[0])
                nc.scalar.activation(small[:, 1, :], small[:, 0, :], ACT.Sqrt).then_inc(root_out, 1)

            cast(0, 0)
            root()
            cast(0, 1)
            with act.Fori(1, NT // (2 * GRP)) as gg:
                cast(gg, 0)
                cast(gg, 1)
            root()
            root()

            def low_parts(r, scale):
                with act.Fori(0, NT // 2) as h:
                    for u in range(2):
                        act.wait_ge(y_done, h * 2 + (r * NT + u + 1))
                        act.wait_ge(y_free, h * 2 + (r * NT + u + 1))
                        nc.scalar.activation(ylow[:, u, :], psY[u][:, D:2 * D], ACT.Copy,
                                             scale=scale(h * 2 + u)).then_inc(y_low, 1)

            def transposes_out(p, keep=False, hidden=False):
                four, fourT, h2T = fours(p["four"])
                with act.Fori(0, NF // 2) as h:
                    for u in range(2):
                        i = h * 2 + u
                        act.wait_ge(four_T, i + (NF * p["q"] + 1))
                        act.wait_ge(four_mm, i + (NF * p["q"] + 1))
                        nc.scalar.activation(fourT[:, u, :], psC[u], ACT.Copy).then_inc(four_Tc, 1)
                        if keep:
                            nc.scalar.activation(XN[:, bass.ds(i * 4, 4), 0:D], four[:, u, :].rearrange("p (t c) -> p t c", c=D),
                                                 ACT.Copy).then_inc(xn_copied, 1)
                        if hidden:
                            act.wait_ge(h2_done, i + 1)
                            nc.scalar.activation(h2T[:, u, :], psH2[u], ACT.Tanh, bias=bproj_s[:, :]) \
                              .then_inc(h2_act, 1)

            def experts(L):
                act.wait_ge(gate_in, 1 + L["n"])
                nc.scalar.activation(gsmall[:, 1, :], gsmall[:, 0, :], ACT.Exp).then_inc(gate_exp, 1)
                act.wait_ge(eid_ready, 1 + L["n"])

                def hidden(i, s, j):
                    e = act.value_load(eid[0:1, bass.ds(j, 1)], min_val=0, max_val=L["E"] - 1)
                    act.wait_ge(h_done, j + (L["jb"] + 3))
                    for h in range(2):
                        last = nc.scalar.activation(psH[s % 2][:, h, :], psH[s % 2][:, h, :], ACT.Relu,
                                                    scale=1.0 / WSCALE, bias=L["b1T"][:, h, bass.ds(e, 1)])
                    last.then_inc(relu_done, 1)
                    act.wait_ge(relu_done, j + (L["jb"] + 1))
                    act.wait_ge(o_done, j + (L["jb"] + 1))
                    nc.scalar.activation(hTs[:, s % 2, 0, :, :], psH[s % 2], ACT.Copy).then_inc(h_act, 1)

                with act.Fori(0, L["tiles"] // RING) as i:
                    for s in range(RING):
                        hidden(i, s, i * RING + s)

            low_parts(0, lambda t: rsd[:, bass.ds(t, 1)])
            transposes_out(mix)
            root()
            act.wait_ge(pack_out[0][0], 16 + 16 * E0)
            transposes_out(layers[0], keep=True)
            experts(layers[0])
            root()
            act.wait_ge(constants_ready, 1)
            nc.scalar.activation(tanh1[:, :], ones[:, 0:1], ACT.Tanh).then_inc(tanh_ready, 1)
            transposes_out(proj, hidden=True)
            low_parts(1, lambda t: 1.0)
            root()
            transposes_out(layers[1], keep=True)
            experts(layers[1])

        @block.vector
        def _(dve):
            v = nc.vector
            step = Steps(dve, dve_steps)
            dve.sem_inc(chunk_free, NCH)
            dve.sem_inc(words_free, 2)
            dve.sem_inc(y_free, 2)
            dve.sem_inc(four_free, 2)
            dve.sem_inc(o_copied, 2)
            roots = [0]

            def inverse_root(dst, src_op, scale):
                roots[0] += 1
                src_op(small[:, 0, :]).then_inc(root_in, 1)
                dve.wait_ge(root_in, roots[0])
                dve.wait_ge(root_out, roots[0])
                step(v.reciprocal(small[:, 2, :], small[:, 1, :]))
                step(v.tensor_tensor(small[:, 2, :], small[:, 2, :], small[:, 0, :], ALU.mult))
                step(v.tensor_tensor(small[:, 2, :], small[:, 2, :], small[:, 1, :], ALU.add))
                step(v.reciprocal(small[:, 3, :], small[:, 2, :]))
                step(v.tensor_scalar(dst[:, :], small[:, 3, :], 2.0 * scale, None, ALU.mult))

            def norm_stats():
                a, b, c = small[:, 1, :], small[:, 2, :], small[:, 3, :]
                step(v.tensor_tensor(a, stats[:, :, 1], stats[:, :, 4], ALU.add))
                step(v.tensor_scalar(mean[:, :], a, 0.5, None, ALU.mult))
                step(v.tensor_tensor(b, stats[:, :, 1], stats[:, :, 4], ALU.subtract))
                step(v.tensor_tensor(b, b, b, ALU.mult))
                step(v.tensor_tensor(c, stats[:, :, 2], stats[:, :, 5], ALU.add))
                step(v.scalar_tensor_tensor(c, b, D / 4.0, c, ALU.mult, ALU.add))
                inverse_root(rstd, lambda o: v.tensor_scalar(o, c, 1.0 / D, EPS, ALU.mult, ALU.add), 1.0)

            step(v.memset(big1[:, :], 0.0))
            step(v.memset(xr[:, :, :, 0, D + 1:MW], 1.0))
            step(v.memset(xr[:, :, :, 1, D + 1:MW], 0.0))
            dve.wait_ge(x_loaded, 16)
            with dve.Fori(0, NF) as i:
                for j in range(4):
                    last = v.bn_stats(stats[:, bass.ds(i * 4 + j, 1), :].rearrange("p t c -> p (t c)"),
                                      X[:, bass.ds(i * 4 + j, 1), :].rearrange("p t c -> p (t c)"))
                last.then_inc(dve_steps, 1)
            step.n += NF
            dve.wait_ge(dve_steps, step.n)
            norm_stats()
            step(v.tensor_scalar(rstd01[:, :], rstd[:, :], 0.1, None, ALU.mult))
            dve.wait_ge(setup_T, 1)
            dve.wait_ge(constants_ready, 1)
            step(v.scalar_tensor_tensor(wmix[:, :], PS[:, 2, 0:D], 1.0, ident[:, :], ALU.mult, ALU.add))
            step(v.tensor_scalar(wmix[:, :], wmix[:, :], 0.5, None, ALU.mult))
            step(v.tensor_copy(b1T1[:, :, :], PS[:, 3, 0:2 * E1].rearrange("p (h e) -> p h e", h=2)))
            step(v.tensor_tensor(rb0[:, 0, :], rb0[:, 0, :], rb0[:, 1, :], ALU.add))
            v.tensor_copy(b1T0[:, :, :], PS[:, 4, 0:2 * E0].rearrange("p (h e) -> p h e", h=2)).then_inc(setup_used, 1)
            dve.wait_ge(setup_used, 1)

            def group(gg, u, chain):
                g = gg * 2 + u

                n = [0]

                def chained(ins):
                    n[0] += 1
                    ins.then_inc(dve_steps, 1)
                    wait_apart(dve, (dve_steps, chain + n[0]))

                for j in range(GRP):
                    chained(v.tensor_scalar(xf[:, j, :], X[:, bass.ds(g * GRP + j, 1), :].rearrange("p t c -> p (t c)"),
                                            mean[:, bass.ds(g * GRP + j, 1)], rstd[:, bass.ds(g * GRP + j, 1)],
                                            ALU.subtract, ALU.mult))
                wait_apart(dve, (chunk_done, g * NCH + NCH), (cast_done, g * (4 * GRP) + 4 * GRP))
                chained(v.tensor_copy(xr[:, u, :, 0, 0:D], xf[:, :, :]))
                v.tensor_tensor(xr[:, u, :, 1, 0:D], xf[:, :, :], xr[:, u, :, 0, 0:D], ALU.subtract)
                chained(v.reduce_sum(deg[:, bass.ds(g * GRP, GRP)], dpart[:, u, :, :], AX.X))
                chained(v.tensor_copy(xr[:, u, :, 0, D:D + 1].rearrange("p j c -> p (j c)"), deg[:, bass.ds(g * GRP, GRP)]))
                v.tensor_tensor(xr[:, u, :, 1, D:D + 1].rearrange("p j c -> p (j c)"), deg[:, bass.ds(g * GRP, GRP)],
                                xr[:, u, :, 0, D:D + 1].rearrange("p j c -> p (j c)"), ALU.subtract).then_inc(xr_ready, 1)

                def words(w):
                    wait_apart(dve, (words_T, g * 4 + w + 1))
                    v.tensor_copy(adjT[:, bass.ds(g * GRP + w // 2, 1), (w % 2) * 1024:(w % 2 + 1) * 1024]
                                  .rearrange("p t w -> p (t w)"),
                                  PS[:, w % 2, :].bitcast(u16)).then_inc(words_free, 1)

                def sums(c):
                    n = min(CH, 2 * NK - CH * c)
                    dve.wait_ge(chunk_done, g * NCH + (2 * NCH + c + 1))
                    dve.wait_ge(chunk_free, g * NCH + c + 1)
                    v.tensor_tensor(msum[:, CH * c:CH * c + n, :], psM[c % 6][:, 0:n, :],
                                    msum[:, CH * c:CH * c + n, :], ALU.add).then_inc(chunk_free, 1)

                for kind, i in ORDER:
                    (words if kind == "T" else sums)(i)

            base = step.n
            with dve.Fori(0, NT // (2 * GRP)) as gg:
                group(gg, 0, gg * 10 + base)
                group(gg, 1, gg * 10 + (base + 5))
            step.n = base + 10 * (NT // (2 * GRP))
            dve.wait_ge(chunk_free, NCH * (NT // GRP) + NCH)
            dve.wait_ge(xr_ready, NT // GRP)
            dve.sem_inc(deg_ready, 1)

            inverse_root(rsd, lambda o: v.tensor_copy(o, deg[:, :]), 0.9)
            step(v.reciprocal(small[:, 2, :], msum[:, :, D + 1]))
            inverse_root(redge, lambda o: v.tensor_tensor(o, msum[:, :, D], small[:, 2, :], ALU.mult), 1.0)
            for b in range(4):
                e = slice(8 * b, 8 * b + 8)
                step(v.tensor_tensor(msum[:, e, 0:D], msum[:, e, 0:D],
                                     redge[:, e].unsqueeze(2).to_broadcast((P, 8, D)), ALU.mult))
                step(v.tensor_copy(Z[:, e, 0:D], msum[:, e, 0:D]))
                v.tensor_tensor(Z[:, e, D:2 * D], msum[:, e, 0:D], Z[:, e, 0:D], ALU.subtract).then_inc(z_ready, 1)
            dve.wait_ge(z_ready, 4)

            def product(r, post, k):
                def copy_block(t, u):
                    v.tensor_copy(block_words[:, u, :], adjT[:, bass.ds(t, 1), :].rearrange("p t w -> p (t w)")) \
                     .then_inc(blk_ready, 1)

                def after(t, u, n):
                    dve.wait_ge(y_done, t + (r * NT + 1))
                    dve.wait_ge(y_low, t + (r * NT + 1))
                    post(t, u, n)

                base = step.n
                copy_block(0, 0)
                copy_block(1, 1)
                with dve.Fori(0, NT // 2 - 1) as h:
                    for u in range(2):
                        after(h * 2 + u, u, h * (2 * k) + (base + u * k))
                        copy_block(h * 2 + u + 2, u)
                for u in range(2):
                    after(NT - 2 + u, u, base + (NT - 2 + u) * k)
                step.n = base + NT * k

            def tile_of(a, t):
                return a[:, bass.ds(t, 1), :].rearrange("p t c -> p (t c)")

            def mixed(t, u, n):
                step.n = n
                v.scalar_tensor_tensor(ysum[:, u, :], psY[u][:, 0:D], rsd[:, bass.ds(t, 1)], ylow[:, u, :],
                                       ALU.mult, ALU.add).then_inc(y_free, 1)
                step(v.tensor_scalar(tile_of(comb, t), tile_of(X, t), mean[:, bass.ds(t, 1)], rstd01[:, bass.ds(t, 1)],
                                     ALU.subtract, ALU.mult))
                step(v.tensor_tensor(tile_of(comb, t), tile_of(comb, t), ysum[:, u, :], ALU.add))

            product(0, mixed, 2)

            def pass_fours(p, fill, use):
                def use_i(i, u):
                    dve.wait_ge(four_mm, i + (NF * p["q"] + 3))
                    use(i, u)

                fill_ahead(dve, fill, use_i)

            four, fourT, h2T = fours(big3)

            def fill_mix(i, u):
                v.tensor_copy(four[:, u, :], comb[:, bass.ds(i * 4, 4), :].rearrange("p t c -> p (t c)")) \
                 .then_inc(four_ready, 1)

            def use_mix(i, u):
                flat = X[:, bass.ds(i * 4, 4), :].rearrange("p t c -> p (t c)")
                v.tensor_tensor(flat, flat, psR[u], ALU.add).then_inc(four_free, 1)
                dve.wait_ge(four_free, i + 3)
                for j in range(4):
                    last = v.bn_stats(stats[:, bass.ds(i * 4 + j, 1), :].rearrange("p t c -> p (t c)"),
                                      tile_of(X, i * 4 + j))
                last.then_inc(dve_steps, 1)

            def fill_norm(p):
                four, _, _ = fours(p["four"])

                def fill(i, u):
                    for j in range(4):
                        last = v.tensor_scalar(four[:, u, j * D:(j + 1) * D], tile_of(X, i * 4 + j),
                                               mean[:, bass.ds(i * 4 + j, 1)], rstd[:, bass.ds(i * 4 + j, 1)],
                                               ALU.subtract, ALU.mult)
                    last.then_inc(four_ready, 1)
                return fill

            dve.wait_ge(prefilled, 16 * (T1 // NT))
            pass_fours(mix, fill_mix, use_mix)
            step.n += NF
            dve.wait_ge(dve_steps, step.n)
            norm_stats()

            def use_router(L):
                E = L["E"]
                four, _, _ = fours(L["four"])
                bias = rb0[:, 0, :] if L["n"] == 0 else rb1[:, :]
                base = step.n

                def use(i, u):
                    step.n = i * 3 + base
                    dve.wait_ge(xn_copied, i + (NF * L["n"] + 1))
                    v.tensor_tensor(XN[:, bass.ds(i * 4, 4), D:2 * D], four[:, u, :].rearrange("p (t c) -> p t c", c=D),
                                    XN[:, bass.ds(i * 4, 4), 0:D], ALU.subtract).then_inc(xn_ready, 1)
                    dve.wait_ge(dve_steps, step.n)
                    l3 = l4[:, :, 0:E]
                    v.tensor_tensor(l3, psR[u][:, 0:4 * E].rearrange("p (t e) -> p t e", t=4),
                                    bias.unsqueeze(1).to_broadcast((P, 4, E)), ALU.add).then_inc(four_free, 1)
                    wait_apart(dve, (four_free, i + (NF * L["q"] + 3)))
                    for j in range(4):
                        last = v.max(out=top[:, j, :], in_=l4[:, j, 0:E])
                    step(last, alone=True)
                    for j in range(4):
                        last = v.max_index(topi[:, j, :], top[:, j, :], l4[:, j, 0:E])
                    step(last, alone=True)
                    v.tensor_copy(val12[:, bass.ds(i * 4, 4), :], top[:, :, 0:2])
                    step(v.tensor_copy(idx12[:, bass.ds(i * 4, 4), :], topi[:, :, 0:2]))
                pass_fours(L, fill_norm(L), use)
                step.n = base + 3 * NF

            def route(L):
                E, n, part = L["E"], L["n"], L["part"]
                et = lambda a: a.rearrange("p (e t) -> p e t", t=NT)
                over_t = lambda a: a.unsqueeze(2).to_broadcast((P, E, NT))
                over_e = lambda a: a.unsqueeze(1).to_broadcast((P, E, NT))
                for k in range(2):
                    step(v.tensor_tensor(et(L["oh"][k]), over_t(iotaE[:, 0:E]), over_e(idx12[:, :, k]), ALU.is_equal))
                v.tensor_tensor(L["both"], L["oh"][0], L["oh"][1], ALU.add).then_inc(cnt_ready, 1)
                v.tensor_tensor(gsmall[:, 0, :], val12[:, :, 1], val12[:, :, 0], ALU.subtract).then_inc(gate_in, 1)
                dve.wait_ge(cnt_done, 1 + n)
                w = E * NT
                tot, rank = banks[:, 0:w], banks[:, 2048:2048 + w]
                run, excl, a, b = part[3], part[4], part[5], part[6]
                step(v.tensor_tensor_scan(run, zero1[:, :].to_broadcast((P, w)), tot, 0.0, ALU.add, ALU.add))
                step(v.tensor_tensor(excl, run, tot, ALU.subtract))
                count, tiles, upto, begin, shift = (expt[:, i, 0:E] for i in range(5))
                first = et(excl)[:, :, 0]
                step(v.tensor_tensor(count, et(run)[:, :, NT - 1], first, ALU.subtract))
                step(v.tensor_tensor(et(a), over_t(count), over_e(step128[:, :]), ALU.is_gt))
                step(v.reduce_sum(tiles, et(a), AX.X))
                step(v.tensor_tensor_scan(upto, zero1[:, :].to_broadcast((P, E)), tiles, 0.0, ALU.add, ALU.add))
                step(v.tensor_tensor(part[2][:, 0:E], upto, iotaP[:, :].to_broadcast((P, E)), ALU.is_le))
                step(v.reduce_sum(eidc[:, :], part[2][:, 0:E], AX.X))
                v.tensor_scalar(eidc[:, :], eidc[:, :], float(E - 1), None, ALU.min).then_inc(eid_col, 1)
                step(v.tensor_tensor(begin, upto, tiles, ALU.subtract))
                step(v.scalar_tensor_tensor(shift, begin, float(P), first, ALU.mult, ALU.subtract))
                dve.wait_ge(eid_row, 1 + n)
                v.tensor_copy(eid[:, :], PS[0:1, 0, 0:P]).then_inc(eid_ready, 1)
                step(v.tensor_tensor(et(a), et(excl), over_t(shift), ALU.add))
                step(v.tensor_tensor(a, a, rank, ALU.add))
                for k in range(2):
                    step(v.tensor_tensor(b, L["oh"][k], a, ALU.mult))
                    step(v.reduce_sum(posf[:, k, :], b.rearrange("p (e t) -> p t e", t=NT), AX.X))
                v.tensor_copy(pos[:, :, :], posf[:, :, :]).then_inc(pos_ready, 1)
                dve.wait_ge(gate_exp, 1 + n)
                step(v.tensor_scalar(gsmall[:, 0, :], gsmall[:, 1, :], 1.0, None, ALU.add))
                step(v.reciprocal(gate[:, 0, :], gsmall[:, 0, :]))
                step(v.tensor_tensor(gate[:, 1, :], gate[:, 0, :], gsmall[:, 1, :], ALU.mult))

            def expert_loop(L):
                jb = L["jb"]
                dve.wait_ge(b2_loaded, 16 * (1 + L["n"]))
                dve.wait_ge(eid_ready, 1 + L["n"])

                def turned(s, j):
                    wait_apart(dve, (xT_done, j + (jb + 1)), (h_done, j + (jb + 1)))
                    v.tensor_copy(xTs[:, s % 2, :, :], psX[s % 2]).then_inc(xT_copied, 1)

                def low(s, j):
                    dve.wait_ge(h_act, j + (jb + 1))
                    v.tensor_tensor(hTs[:, s % 2, 1, :, :], psH[s % 2], hTs[:, s % 2, 0, :, :], ALU.subtract) \
                     .then_inc(split_low, 1)

                def result(i, s, j):
                    e = dve.value_load(eid[0:1, bass.ds(j, 1)], min_val=0, max_val=L["E"] - 1)
                    dve.wait_ge(o_done, j + (jb + 3))
                    if s % XG == 0:
                        dve.wait_ge(stored[s // XG], i * 16 + (16 * (jb // RING) + 16))
                    v.scalar_tensor_tensor(yss[:, s // XG, s % XG, :], psO[s % 2], 1.0 / WSCALE, L["b2s"][:, bass.ds(e * D, D)],
                                           ALU.mult, ALU.add) \
                     .then_inc(o_copied, 1)

                turned(0, 0)

                def body(i, s, j):
                    if not isinstance(j, int) or j + 1 < L["tiles"]:
                        turned((s + 1) % RING, j + 1)
                    if not isinstance(j, int) or j >= 1:
                        low((s - 1) % RING, j - 1)
                    if not isinstance(j, int) or j >= 2:
                        result(i if s >= 2 else i - 1, (s - 2) % RING, j - 2)
                ring_rounds(dve, L["tiles"], body)
                low(RING - 1, L["tiles"] - 1)
                for s in (RING - 2, RING - 1):
                    result(L["tiles"] // RING - 1, s, L["tiles"] - RING + s)

            def combine(L):
                n = L["n"]
                for b in range(NF):
                    t = slice(4 * b, 4 * b + 4)
                    dve.wait_ge(gathered[b], 128 * (n + 1))
                    for k in range(2):
                        step(v.tensor_tensor(gath[k][:, t, :], gath[k][:, t, :],
                                             gate[:, k, t].unsqueeze(2).to_broadcast((P, 4, D)), ALU.mult))
                    step(v.tensor_tensor(gath[0][:, t, :], gath[0][:, t, :], gath[1][:, t, :], ALU.add))
                    v.tensor_tensor(X[:, t, :], X[:, t, :], gath[0][:, t, :], ALU.add).then_inc(combined, 1)
                    if n == 0:
                        dve.wait_ge(combined, b + 1)
                        for tt in range(4 * b, 4 * b + 4):
                            last = v.bn_stats(stats[:, tt, :], X[:, tt, :])
                        step(last)

            use_router(layers[0])
            route(layers[0])
            expert_loop(layers[0])
            combine(layers[0])
            norm_stats()

            dve.wait_ge(cut_flag, 1)
            with dve.Fori(0, NT) as t:
                n = dve.value_load(cuti[0:1, bass.ds(t, 1)], min_val=0, max_val=N)
                wait_apart(dve, (cut_loaded, t * 16 + 16))
                with dve.If(n > KEEP):
                    v.tensor_tensor_scan(cut_count, zero1[:, :].to_broadcast((P, N)), cut_rows, 0.0, ALU.add, ALU.add) \
                     .then_inc(dve_steps, 1)
                    wait_apart(dve, (dve_steps, t + (step.n + 1)))
                    v.scalar_tensor_tensor(cut_nat, cut_count, float(KEEP), cut_rows, ALU.is_le, ALU.mult, saturate=False) \
                     .then_inc(cut_masked, 1)
                with dve.Else():
                    dve.sem_inc(dve_steps, 1)
                    dve.sem_inc(cut_masked, 1)
                wait_apart(dve, (cut_T, t + 1))
                with dve.If(n > KEEP):
                    v.tensor_copy(adjT[:, bass.ds(t, 1), 0:1024].rearrange("p t w -> p (t w)"), PS[:, 0, :].bitcast(u16))
                    v.tensor_copy(adjT[:, bass.ds(t, 1), 1024:2048].rearrange("p t w -> p (t w)"), PS[:, 1, :].bitcast(u16)) \
                     .then_inc(cut_put, 1)
                with dve.Else():
                    dve.sem_inc(cut_put, 1)
            step.n += NT
            dve.wait_ge(cut_put, NT)

            dve.wait_ge(tanh_ready, 1)

            def use_proj(i, u):
                e4 = Z[:, bass.ds(i * 4, 4), 0:D]
                l4_ = Z[:, bass.ds(i * 4, 4), D:2 * D]
                src = psR[u].rearrange("p (e c) -> p e c", e=4)
                v.tensor_scalar(e4, src, tanh1[:, :], None, ALU.mult).then_inc(z_ready, 1)
                dve.wait_ge(z_ready, i + 5)
                v.scalar_tensor_tensor(l4_, src, tanh1[:, :], e4, ALU.mult, ALU.subtract).then_inc(four_free, 1)

            pass_fours(proj, fill_norm(proj), use_proj)
            dve.wait_ge(four_free, 2 + 3 * NF)

            def graph2(t, u, n):
                step.n = n
                v.tensor_tensor(ysum[:, u, :], psY[u][:, 0:D], ylow[:, u, :], ALU.add).then_inc(y_free, 1)
                dve.wait_ge(y_free, t + (NT + 3))
                step(v.tensor_tensor(ysum[:, u, :], ysum[:, u, :], bgcn_s[:, :], ALU.add))
                step(v.scalar_tensor_tensor(tile_of(X, t), ysum[:, u, :], 0.0, tile_of(X, t), ALU.max, ALU.add))
                step(v.bn_stats(stats[:, bass.ds(t, 1), :].rearrange("p t c -> p (t c)"), tile_of(X, t)))

            product(1, graph2, 3)
            norm_stats()
            use_router(layers[1])
            route(layers[1])
            expert_loop(layers[1])
            combine(layers[1])

        @block.tensor
        def _(pe):
            mm = nc.tensor.matmul
            pe.sem_inc(chunk_done, 2 * NCH)
            pe.sem_inc(four_mm, 2)
            pe.sem_inc(h_done, 2)
            pe.sem_inc(o_done, 2)
            pe.wait_ge(constants_ready, 1)
            pe.wait_ge(weights_loaded, 16 * 12)
            mm(PS[:, 2, 0:D], wnat, ident[:, :], start=True, stop=True)
            for h in range(2):
                mm(PS[:, 3, h * E1:(h + 1) * E1], b1n1[:, h * P:(h + 1) * P], ident[0:E1, 0:E1], start=True, stop=True)
            for h in range(2):
                last = mm(PS[:, 4, h * E0:(h + 1) * E0], b1n0[:, h * P:(h + 1) * P], ident[0:E0, 0:E0], start=True, stop=True)
            last.then_inc(setup_T, 1)
            pe.wait_ge(setup_used, 1)

            def turn_words(src, bank, half):
                words = src.bitcast(bf16)
                for k in range(8):
                    last = pe.transpose(psT[bank][:, k, :], words[:, (8 * half + k) * P:(8 * half + k + 1) * P], identb[:, :])
                return last

            def group(gg, u):
                g = gg * 2 + u
                pe.wait_ge(cast_done, g * (4 * GRP) + 4 * GRP)

                def words(w):
                    pe.wait_ge(words_free, g * 4 + w + 1)
                    turn_words(nat[:, u, w // 2, :], w % 2, w % 2).then_inc(words_T, 1)

                def sums(c):
                    n = min(CH, 2 * NK - CH * c)
                    wait_apart(pe, (chunk_free, g * NCH + (NCH + c - 5 if c >= 6 else c + 7 if c <= 4 else 6)),
                               (xr_ready, g + 1))
                    for e in range(n):
                        k, b = divmod(CH * c + e, 2)
                        for j in range(GRP):
                            a = nat[:, u, j, 256 * k + b:256 * (k + 1):2]
                            mm(psM[c % 6][:, e, :], a, xr[:, u, j, 0, :], start=(j == 0), stop=False)
                            last = mm(psM[c % 6][:, e, :], a, xr[:, u, j, 1, :], start=False, stop=(j == GRP - 1))
                    last.then_inc(chunk_done, 1)

                for kind, i in ORDER:
                    (words if kind == "T" else sums)(i)

            with pe.Fori(0, NT // (2 * GRP)) as gg:
                group(gg, 0)
                group(gg, 1)

            def product(r):
                with pe.Fori(0, NT // 2) as h:
                    for u in range(2):
                        t = h * 2 + u
                        wait_apart(pe, (blk_ready, t + (r * NT + 1)), (y_free, t + (r * NT + 1)))
                        for k in range(NK):
                            for b in range(2):
                                last = mm(psY[u], block8[:, u, k, :, b], Z[:, 2 * k + b, :],
                                          start=(k == 0 and b == 0), stop=(k == NK - 1 and b == 1))
                        last.then_inc(y_done, 1)

            def pass_fours(p, final):
                four, fourT, h2T = fours(p["four"])

                def turn(i, u):
                    pe.wait_ge(four_ready, i + (NF * p["q"] + 1))
                    for j in range(4):
                        last = pe.transpose(psC[u][:, j * P:(j + 1) * P], four[:, u, j * D:(j + 1) * D], ident[:, :])
                    last.then_inc(four_T, 1)

                def use(i, u):
                    pe.wait_ge(four_Tc, i + (NF * p["q"] + 1))
                    pe.wait_ge(four_free, i + (NF * p["q"] + 1))
                    final(i, u, fourT[:, u, :], h2T[:, u, :]).then_inc(four_mm, 1)

                fill_ahead(pe, turn, use)

            def by_tile(w, n):
                def final(i, u, fT, hT):
                    for j in range(4):
                        last = mm(psR[u][:, j * n:(j + 1) * n], fT[:, j * P:(j + 1) * P], w, start=True, stop=True)
                    return last
                return final

            def projected(i, u, fT, hT):
                mm(psH2[u], wproj_s[:, :], fT, start=True, stop=True).then_inc(h2_done, 1)
                pe.wait_ge(h2_act, i + 1)
                for k in range(2):
                    for b in range(2):
                        q = 2 * k + b
                        last = mm(psR[u][:, q * D:(q + 1) * D], hT[:, 256 * k + b:256 * (k + 1):2], wgcn_s[:, :],
                                  start=True, stop=True)
                return last

            def experts(L):
                E, jb = L["E"], L["jb"]
                w = E * NT
                pe.wait_ge(cnt_ready, 1 + L["n"])
                for m, at in ((ones, 0), (before, 2048)):
                    for c in range(0, w, 512):
                        n = min(512, w)
                        last = mm(banks[:, at + c:at + c + n], m[:, :], L["both"][:, c:c + n], start=True, stop=True)
                last.then_inc(cnt_done, 1)
                pe.wait_ge(eid_col, 1 + L["n"])
                mm(PS[0:1, 0, 0:P], eidc[:, :], ident[:, :], start=True, stop=True).then_inc(eid_row, 1)
                pe.wait_ge(pos_ready, 1 + L["n"])

                def turn(i, s, j):
                    if s % XG == 0:
                        wait_apart(pe, (tokens_in[s // XG], i * 16 + (16 * (jb // RING) + 16)))
                    for q in range(2):
                        last = pe.transpose(psX[s % 2][:, q, :], xss[:, s // XG, s % XG, q * D:(q + 1) * D], identh[:, :])
                    last.then_inc(xT_done, 1)

                def split(out, a, b):
                    mm(out, a[0], b[0], start=a[2], stop=False)
                    mm(out, a[0], b[1], start=False, stop=False)
                    return mm(out, a[1], b[0], start=False, stop=a[3])

                def hidden(i, s, j):
                    pe.wait_ge(weights_in[s], i * 16 + (16 * (jb // RING) + 16))
                    pe.wait_ge(xT_copied, j + (jb + 1))
                    for h in range(2):
                        hi, lo = (w1s[:, s, q, h * P:(h + 1) * P] for q in (0, 1))
                        last = split(psH[s % 2][:, h, :], (hi, lo, True, True), (xTs[:, s % 2, 0, :], xTs[:, s % 2, 1, :]))
                    last.then_inc(h_done, 1)

                def result(s, j):
                    pe.wait_ge(split_low, j + (jb + 1))
                    pe.wait_ge(o_copied, j + (jb + 1))
                    for h in range(2):
                        hi, lo = (hTs[:, s % 2, q, h, :] for q in (0, 1))
                        whi, wlo = (w2s[:, s, q, h * D:(h + 1) * D] for q in (0, 1))
                        last = split(psO[s % 2], (hi, lo, h == 0, h == 1), (whi, wlo))
                    last.then_inc(o_done, 1)

                turn(0, 0, 0)

                def body(i, s, j):
                    if not isinstance(j, int) or j + 1 < L["tiles"]:
                        turn(i if s + 1 < RING else i + 1, (s + 1) % RING, j + 1)
                    if not isinstance(j, int) or j >= 2:
                        result((s - 2) % RING, j - 2)
                    hidden(i, s, j)
                ring_rounds(pe, L["tiles"], body)
                for s in (RING - 2, RING - 1):
                    result(s, L["tiles"] - RING + s)

            pe.wait_ge(z_ready, 4)
            product(0)
            pass_fours(mix, by_tile(wmix[:, :], D))
            pass_fours(layers[0], by_tile(wr0_s[:, :], E0))
            experts(layers[0])
            pe.wait_ge(cut_flag, 1)
            with pe.Fori(0, NT) as t:
                n = pe.value_load(cuti[0:1, bass.ds(t, 1)], min_val=0, max_val=N)
                pe.wait_ge(cut_masked, t + 1)
                with pe.If(n > KEEP):
                    turn_words(cut_nat, 0, 0)
                    turn_words(cut_nat, 1, 1).then_inc(cut_T, 1)
                with pe.Else():
                    pe.sem_inc(cut_T, 1)
            pass_fours(proj, projected)
            pe.wait_ge(z_ready, 4 + NF)
            product(1)
            pass_fours(layers[1], by_tile(wr1_s[:, :], E1))
            experts(layers[1])


_INS = ['x', 'adj', 'L0_gnn_W', 'L0_ffn_Wg', 'L0_ffn_bg', 'L0_ffn_bias', 'L0_ffn_W1', 'L0_ffn_b1', 'L0_ffn_W2',
        'L0_ffn_b2', 'L1_gnn_W_proj', 'L1_gnn_b_proj', 'L1_gnn_W_gcn', 'L1_gnn_b_gcn', 'L1_ffn_Wr', 'L1_ffn_br',
        'L1_ffn_W1', 'L1_ffn_b1', 'L1_ffn_W2', 'L1_ffn_b2']


def kernel(**inputs):
    import numpy as np
    import concourse.bacc as bacc
    from concourse.bass_utils import run_bass_kernel_spmd as run

    nc = bacc.Bacc("TRN2", target_bir_lowering=False, num_devices=1)
    arrays, args = {}, []
    for name in _INS:
        a = np.ascontiguousarray(inputs[name])
        arrays[f"in_{name}"] = a
        args.append(nc.dram_tensor(f"in_{name}", a.shape, mybir.dt.from_np(a.dtype), kind="ExternalInput").ap())
    args.append(nc.dram_tensor("out_0", (N, D), mybir.dt.float32, kind="ExternalOutput").ap())
    program(nc, *args)
    r = run(nc, [arrays], core_ids=[0])
    return r.results[0]["out_0"]
```

```python
from contextlib import ExitStack

import concourse.bass as bass
from concourse import mybir

N, D, HID = 4096, 128, 256
P = 128
NT = N // P
NK = N // 256
E0, E1 = 8, 64
KEEP = 350
NG = 4
EPS = 1e-5
DEEP = 28
GRP = 2
CH = 3
NCH = -(-2 * NK // CH)
MW = D + 2
RING = 8
XG = 4
XW = 2 * D + 2
WSCALE = 64.0
WW = 2 * HID
ORDER = [("T", 0), ("T", 1), ("C", 0), ("C", 1), ("C", 2), ("T", 2), ("C", 3), ("C", 4), ("C", 5), ("T", 3)] + \
        [("C", c) for c in range(6, NCH)]


def slot_tiles(n_experts):
    need = 2 * N // P + n_experts - 1
    return -(-need // RING) * RING


def program(nc, x, adj, w_gnn0, wg, bg, bias0, w1_0, b1_0, w2_0, b2_0,
            w_proj, b_proj, w_gcn, b_gcn, wr, br, w1_1, b1_1, w2_1, b2_1, out):
    f32, f16, bf16 = mybir.dt.float32, mybir.dt.float16, mybir.dt.bfloat16
    f8, u16, i32, u32 = mybir.dt.float8e4, mybir.dt.uint16, mybir.dt.int32, mybir.dt.uint32
    ALU, ACT, AX = mybir.AluOpType, mybir.ActivationFunctionType, mybir.AxisListType
    ctx = ExitStack()
    with ctx:
        def sb(name, shape, dt):
            return ctx.enter_context(nc.sbuf_tensor(name, shape, dt))

        def sem(name):
            return ctx.enter_context(nc.semaphore(name))

        slots_dram = [nc.dram_tensor(f"slots{n}", (slot_tiles(E) * P, XW), f16, kind="Internal").ap()
                      for n, E in ((0, E0), (1, E1))]
        results_dram = nc.dram_tensor("results", (2 * N + RING * P, D), f32, kind="Internal").ap()
        packed_dram = [nc.dram_tensor(f"packed{n}", (E * P, 2 * WW), f16, kind="Internal").ap()
                       for n, E in ((0, E0), (1, E1))]

        adjT = sb("adjT", [P, NT, NK * P], u16)
        big1 = sb("big1", [P, 2 * NK * MW], f32)
        big2 = sb("big2", [P, NT * XW // 2], f32)
        big3 = sb("big3", [P, N], f32)
        X = sb("X", [P, NT, D], f32)
        adj_words = adjT[:, :, :].rearrange("p t w -> p (t w)").bitcast(f32)
        msum = big1[:, :].rearrange("p (e c) -> p e c", c=MW)
        comb = big1[:, 0:N].rearrange("p (t c) -> p t c", c=D)
        gath = [big2[:, 0:N].rearrange("p (t c) -> p t c", c=D), comb]
        stage = [big2[:, 0:N].rearrange("p (s c) -> p s c", s=4),
                 adj_words[:, (NT - 4) * 1024:NT * 1024].rearrange("p (s c) -> p s c", s=4)]
        XN = big2[:, :].bitcast(f16).rearrange("p (t c) -> p t c", c=XW)
        XN_row = big2[:, :].bitcast(i32).rearrange("p (t c) -> p t c", c=XW // 2)[:, :, D]
        blank = big2[:, 2048:2048 + RING * XW // 2].rearrange("p (s c) -> p s c", s=RING)
        nat = big3[:, :].bitcast(f8).rearrange("p (u j e) -> p u j e", u=2, j=GRP)
        Z = big3[:, :].bitcast(f16).rearrange("p (e c) -> p e c", c=2 * D)
        block_words = big2[:, 0:NK * P].bitcast(u16).rearrange("p (u w) -> p u w", u=2)
        block8 = big2[:, 0:NK * P].bitcast(f8).rearrange("p (u k n b) -> p u k n b", u=2, k=NK, b=2)
        cut_rows, cut_count = big3[:, :], big1[:, 1024:1024 + N // 2]
        cut_nat = big1[:, 0:N // 4].bitcast(f8)
        ws = big3[:, :].bitcast(f16).rearrange("p (s c) -> p s c", s=RING)
        w1s = ws.rearrange("p s (l c) -> p s l c", l=2)[:, :, :, 0:HID]
        w2s = ws.rearrange("p s (l c) -> p s l c", l=2)[:, :, :, HID:2 * HID]
        xss_words = big1[:, 0:XG * XW]
        xss = xss_words.bitcast(f16).rearrange("p (g s c) -> p g s c", g=2, s=XG)
        xss_row = xss_words.bitcast(i32).rearrange("p (g s c) -> p g s c", g=2, s=XG)[:, :, :, D]
        rows = big1[:, 2824:2824 + 2 * XG].bitcast(i32).rearrange("p (g s) -> p g s", g=2)
        yss = big1[:, 1032:1032 + 2 * XG * D].rearrange("p (g s c) -> p g s c", g=2, s=XG)
        hTs = big2[:, 0:4 * 256].bitcast(f16).rearrange("p (s l h n) -> p s l h n", s=4, l=2, h=2)
        xTs = big1[:, 2568:2568 + 256].bitcast(f16).rearrange("p (s l n) -> p s l n", s=2, l=2)

        def fours(big):
            v = big[:, 0:6 * 4 * D].rearrange("p (a u c) -> p a u c", a=3, u=2)
            return v[:, 0], v[:, 1], v[:, 2]

        ident = sb("ident", [P, P], f32)
        identb = sb("identb", [P, P], bf16)
        identh = sb("identh", [P, P], f16)
        before = sb("before", [P, P], bf16)
        ones = sb("ones", [P, P], bf16)
        iotaE = sb("iotaE", [P, E1], f32)
        step128 = sb("step128", [P, NT], f32)
        iotaP = sb("iotaP", [P, 1], f32)
        zero1 = sb("zero1", [P, 1], f32)
        wmix = sb("wmix", [P, D], f32)
        wproj_s = sb("wproj_s", [P, D], f32)
        wgcn_s = sb("wgcn_s", [P, D], f32)
        wr0_s = sb("wr0_s", [P, E0], f32)
        wr1_s = sb("wr1_s", [P, E1], f32)
        rb0 = sb("rb0", [P, 2, E0], f32)
        rb1 = sb("rb1", [P, E1], f32)
        bproj_s = sb("bproj_s", [P, 1], f32)
        bgcn_s = sb("bgcn_s", [P, D], f32)
        b1T0 = sb("b1T0", [P, 2, E0], f32)
        b1T1 = sb("b1T1", [P, 2, E1], f32)
        xr = sb("xr", [P, 2, GRP, 2, MW], f16)
        xf = sb("xf", [P, GRP, D], f32)
        dpart = sb("dpart", [P, 2, GRP, 4], f32)
        degx = sb("degx", [P, NT + NG], f32)
        deg = degx[:, 0:NT]
        rsd = sb("rsd", [P, NT], f32)
        redge = sb("redge", [P, NT], f32)
        small = sb("small", [P, 4, NT], f32)
        gsmall = sb("gsmall", [P, 2, NT], f32)
        stats = sb("stats", [P, NT, 6], f32)
        mean = sb("mean", [P, NT], f32)
        rstd = sb("rstd", [P, NT], f32)
        rstd01 = sb("rstd01", [P, NT], f32)
        l4 = sb("l4", [P, 4, E1], f32)
        top = sb("top", [P, 4, 8], f32)
        topi = sb("topi", [P, 4, 8], u32)
        val12 = sb("val12", [P, NT, 2], f32)
        idx12 = sb("idx12", [P, NT, 2], f32)
        gate = sb("gate", [P, 2, NT], f32)
        posf = sb("posf", [P, 2, NT], f32)
        pos = sb("pos", [P, 2, NT], i32)
        expt = sb("expt", [P, 5, E1], f32)
        eidc = sb("eidc", [P, 1], f32)
        eid = sb("eid", [1, P], i32)
        tanh1 = sb("tanh1", [P, 1], f32)
        ysum = big2[:, 3616:3872].rearrange("p (u c) -> p u c", u=2)
        ylow = big2[:, 3872:4128].rearrange("p (u c) -> p u c", u=2)
        degmax = sb("degmax", [P, NT + NG], f32)
        cuti = sb("cuti", [1, NT + NG], i32)
        carry = sb("carry", [P, 1], f32)
        wnat = adj_words[:, 0:D]
        b1n1 = adj_words[0:E1, 128:128 + HID]
        b1n0 = adj_words[0:E0, 384:384 + HID]
        tokens = sb("tokens", [P, NT], i32)
        iotas = adj_words[:, 1024:1024 + E1 + NT + 1].bitcast(i32)

        PS = ctx.enter_context(nc.psum_tensor("PS", [P, 8, 512], f32))
        psT = [PS[:, b, :].bitcast(bf16).rearrange("p (k n) -> p k n", n=P) for b in range(2)]
        psM = [PS[:, 2 + b, 0:CH * MW].rearrange("p (e c) -> p e c", c=MW) for b in range(6)]
        psY = [PS[:, b, 0:2 * D] for b in range(2)]
        psC = [PS[:, 2 + b, :] for b in range(2)]
        psR = [PS[:, 4 + b, :] for b in range(2)]
        psH2 = [PS[:, 6 + b, :] for b in range(2)]
        psX = [PS[:, b, 0:P].bitcast(f16).rearrange("p (l n) -> p l n", l=2) for b in range(2)]
        psH = [PS[:, b, 0:2 * P].rearrange("p (h n) -> p h n", h=2) for b in (2, 3, 6, 7)]
        psO = [PS[:, 4 + b, 0:D] for b in range(2)]
        banks = PS[:, :, :].rearrange("p b c -> p (b c)")

        x_loaded, weights_loaded, constants_ready = sem("x_loaded"), sem("weights_loaded"), sem("constants_ready")
        setup_T, setup_used = sem("setup_T"), sem("setup_used")
        arrived = [[sem(f"quarter{s}_{kind}_arrived") for s in range(4)] for kind in ("even", "odd")]
        cast_done = sem("quarter_cast")
        words_T, words_free = sem("words_transposed"), sem("words_bank_free")
        chunk_done, chunk_free = sem("chunk_multiplied"), sem("chunk_bank_free")
        xr_ready = sem("group_tokens_ready")
        root_in, root_out = sem("root_input"), sem("root_output")
        z_scaled, z_high, z_ready = sem("operand_scaled"), sem("operand_high_parts"), sem("operand_ready")
        blk_ready, y_done, y_low, y_free = sem("block_ready"), sem("product_done"), sem("product_low_copied"), sem("product_bank_free")
        four_ready, four_T, four_Tc, four_mm, four_free = (sem(n) for n in (
            "four_ready", "four_transposed", "four_T_copied", "four_multiplied", "four_used"))
        xn_copied, h2_done, h2_act = sem("normalized_copied"), sem("h2_multiplied"), sem("h2_active")
        cnt_ready, cnt_done = sem("choices_ready"), sem("counts_done")
        eid_col, eid_row, eid_ready, pos_ready = (sem(n) for n in ("expert_column", "expert_row", "experts_ready", "slots_ready"))
        gate_in, gate_exp = sem("gate_difference"), sem("gate_exp")
        prefilled, b2_loaded = sem("slots_prefilled"), sem("b2_loaded")
        scattered = sem("scattered")
        weights_in = [sem(f"ring{s}_loaded") for s in range(RING)]
        tokens_in = [sem(f"slot_group{s}_loaded") for s in range(2)]
        relu_done, split_low = sem("hidden_relu"), sem("hidden_low")
        pack_in = [[sem(f"experts{n}_{b}_loaded") for b in range(4 if n else 1)] for n in range(2)]
        pack_out = [[sem(f"experts{n}_{b}_stored") for b in range(4 if n else 1)] for n in range(2)]
        pack_done, pack_scaled = sem("expert_packed"), sem("expert_scaled")
        xn_ready = sem("normalized_split")
        xT_done, xT_copied, h_done, h_act, o_done, o_copied = (sem(n) for n in (
            "slot_transposed", "slot_T_copied", "hidden_done", "hidden_active", "result_done", "result_copied"))
        put_back = [sem(f"slot_group{s}_put_back") for s in range(2)]
        slots_known = sem("choice_slots_known")
        rows_copied, rows_cleared = sem("rows_copied"), sem("blank_ready")
        gathered = [sem(f"gathered{b}") for b in range(NT // 4)]
        combined, out_written = sem("combined"), sem("output_written")
        deg_ready, cut_flag, cut_loaded, cut_masked, cut_T, cut_put = (sem(n) for n in (
            "degrees_ready", "cut_flags", "cut_rows_loaded", "cut_masked", "cut_transposed", "cut_put"))
        tanh_ready = sem("tanh1_ready")
        dve_steps, pool_steps = sem("dve_steps"), sem("pool_steps")

        wait_regs = {}

        def wait_apart(eng, *waits):
            regs = wait_regs.setdefault(eng.engine, [])
            while len(regs) < len(waits):
                regs.append(eng.alloc_register(f"awaited{len(regs)}"))
            for (_, n), reg in zip(waits, regs):
                eng.reg_mov(reg, n)
            eng.wait_ge(constants_ready, 1)
            for (s, _), reg in zip(waits, regs):
                eng.wait_ge(s, reg)

        class Steps:

            def __init__(self, eng, s):
                self.eng, self.sem, self.n = eng, s, 0

            def __call__(self, ins, alone=False):
                self.n = self.n + 1
                ins.then_inc(self.sem, 1)
                if alone:
                    wait_apart(self.eng, (self.sem, self.n))
                else:
                    self.eng.wait_ge(self.sem, self.n)

        T0, T1 = slot_tiles(E0), slot_tiles(E1)
        PREFILLS = 16 * (T0 + T1 + 2 * NT) // RING
        layers = [
            dict(n=0, E=E0, wr=wr0_s, w1=w1_0, w2=w2_0, b2=b2_0, b1T=b1T0, tiles=T0, jb=0, tmp=big1[:, :],
                 b2s=big1[:, 3072:3072 + E0 * D], four=big3, q=1, pack=big2[:, 2048:3072], nb=1),
            dict(n=1, E=E1, wr=wr1_s, w1=w1_1, w2=w2_1, b2=b2_1, b1T=b1T1, tiles=T1, jb=T0, tmp=adj_words,
                 b2s=adj_words[:, 20480:20480 + E1 * D], four=big3, q=3, pack=big1[:, 0:4096], nb=4),
        ]
        for L in layers:
            w = L["E"] * NT
            L["part"] = [L["tmp"][:, i * w:(i + 1) * w] for i in range(8)]
            L["oh"] = [L["part"][0].bitcast(bf16)[:, k * w:(k + 1) * w] for k in (0, 1)]
            L["both"] = L["part"][1].bitcast(bf16)[:, 0:w]
            v_ = L["pack"].rearrange("p (b c) -> p b c", b=L["nb"])
            L["pack32"], L["pack16"] = v_[:, :, 0:WW], v_[:, :, WW:2 * WW]
        def packed(L, b):
            return (L["pack16"][:, b, :].bitcast(f16)[:, q * WW:(q + 1) * WW] for q in (0, 1))

        mix = dict(q=0, four=big3)
        proj = dict(q=2, four=big2)
        NF = NT // 4

        def ring_rounds(eng, tiles, body):
            for s in range(RING):
                body(0, s, s)
            with eng.Fori(1, tiles // RING - 1) as i:
                for s in range(RING):
                    body(i, s, i * RING + s)
            for s in range(RING):
                body(tiles // RING - 1, s, tiles - RING + s)

        def fill_ahead(eng, fill, use):
            fill(0, 0)
            with eng.Fori(0, NF // 2 - 1) as h:
                fill(h * 2 + 1, 1)
                use(h * 2, 0)
                fill(h * 2 + 2, 0)
                use(h * 2 + 1, 1)
            fill(NF - 1, 1)
            use(NF - 2, 0)
            use(NF - 1, 1)

        block = ctx.enter_context(nc.Block())

        @block.sync
        def _(sp):
            for L in layers:
                for b in range(L["nb"]):
                    sp.sem_inc(pack_out[L["n"]][b], 16)
            sp.dma_start(X[:, :, :], x.rearrange("(t p) c -> p t c", p=P)).then_inc(x_loaded, 16)
            for t in range(2):
                for s in range(4):
                    sp.dma_start(stage[t][:, s, :], adj[t * P:(t + 1) * P, s * 1024:(s + 1) * 1024]).then_inc(arrived[t][s], 16)
            row = lambda a, n: a.rearrange("(a n) -> a n", a=1).to_broadcast((P, n))
            for dst, src in (
                    (wnat, w_gnn0), (b1n1, b1_1), (b1n0, b1_0), (wproj_s[:, :], w_proj), (wgcn_s[:, :], w_gcn),
                    (wr0_s[:, :], wg), (wr1_s[:, :], wr), (rb0[:, 0, :], row(bg, E0)), (rb0[:, 1, :], row(bias0, E0)),
                    (rb1[:, :], row(br, E1)), (bproj_s[:, :], b_proj.rearrange("(n a) -> n a", a=1)),
                    (bgcn_s[:, :], row(b_gcn, D))):
                sp.dma_start(dst, src).then_inc(weights_loaded, 16)

            def load_quarter(t, s, kind, used):
                sp.wait_ge(cast_done, used * 4 + (s + 1))
                sp.dma_start(stage[kind][:, s, :], adj[bass.ds(t * P, P), s * 1024:(s + 1) * 1024]) \
                  .then_inc(arrived[kind][s], 16)

            with sp.Fori(0, DEEP // 2 - 1) as h:
                for kind in range(2):
                    for s in range(4):
                        load_quarter(h * 2 + (kind + 2), s, kind, h * 2 + kind)
            for s in range(4):
                load_quarter(DEEP, s, 0, DEEP - 2)
            with sp.Fori(DEEP, NT - 1) as t:
                for s in range(4):
                    load_quarter(t + 1, s, 0, t)

            sp.wait_ge(rows_cleared, 1)
            for dst, tiles in ((slots_dram[0], T0), (slots_dram[1], T1), (results_dram, 2 * NT)):
                width = dst.shape[1] * (2 if dst is results_dram else 1)
                for a in range(0, tiles, RING):
                    part = dst[a * P:(a + RING) * P, :].rearrange("(s p) c -> p s c", p=P)
                    source = blank[:, :, 0:width // 2]
                    sp.dma_start(part, source if dst is results_dram else source.bitcast(f16)).then_inc(prefilled, 16)

            def pack_traffic(L):
                nb, n = L["nb"], L["n"]
                base = n * E0

                def load(e, b):
                    sp.dma_start(L["pack32"][:, b:b + 1, 0:HID], L["w1"][bass.ds(e, 1), :, :].rearrange("e p c -> p e c")) \
                      .then_inc(pack_in[n][b], 16)
                    sp.dma_start(L["pack32"][:, b, HID:2 * HID].rearrange("p (h c) -> p h c", h=2),
                                 L["w2"][bass.ds(e, 1), :, :].rearrange("e (h p) c -> p (e h) c", p=P)) \
                      .then_inc(pack_in[n][b], 16)

                def store(e, b):
                    sp.wait_ge(pack_done, e + (base + 1))
                    sp.dma_start(packed_dram[n][bass.ds(e * P, P), :], L["pack16"][:, b, :].bitcast(f16)) \
                      .then_inc(pack_out[n][b], 16)

                if n == 0:
                    sp.wait_ge(prefilled, PREFILLS)
                else:
                    sp.wait_ge(combined, NF)
                for b in range(nb):
                    load(b, b)
                with sp.Fori(0, L["E"] // nb - 1) as i:
                    for b in range(nb):
                        store(i * nb + b, b)
                        load(i * nb + (b + nb), b)
                for b in range(nb):
                    store(L["E"] - nb + b, b)

            def expert_traffic(L):
                jb, n = L["jb"], L["n"]
                sp.wait_ge(four_free, 2 + NF * (L["q"] + 1))
                sp.wait_ge(xn_ready, 2 + NF * (1 + n))
                if n:
                    sp.wait_ge(y_free, 2 + 2 * NT)
                sp.dma_start(L["b2s"], L["b2"].rearrange("e (a c) -> a (e c)", a=1).to_broadcast((P, L["E"] * D))) \
                  .then_inc(b2_loaded, 16)
                sp.wait_ge(eid_ready, 1 + n)
                if n == 0:
                    cut_traffic()
                for b in range(L["nb"]):
                    sp.wait_ge(pack_out[n][b], 16 + 16 * (L["E"] // L["nb"]))

                def load(s, j):
                    e = sp.value_load(eid[0:1, bass.ds(j, 1)], min_val=0, max_val=L["E"] - 1)
                    sp.dma_start(ws[:, s, :], packed_dram[n][bass.ds(e * P, P), :]).then_inc(weights_in[s], 16)

                for s in range(RING):
                    load(s, s)
                with sp.Fori(0, L["tiles"] // RING - 1) as i:
                    for s in range(RING):
                        if s % 2 == 0:
                            wait_apart(sp, (o_done, i * RING + (s + jb + 6)))
                        load(s, i * RING + (s + RING))

            def results_traffic(L):
                for g in range(2):
                    sp.wait_ge(put_back[g], 16 * XG * ((L["tiles"] + L["jb"]) // RING))
                for b in range(NF):
                    for k in range(2):
                        at = k * N + b * 4 * P
                        sp.dma_start(gath[k][:, 4 * b:4 * b + 4, :],
                                     results_dram[at:at + 4 * P, :].rearrange("(t p) c -> p t c", p=P)).then_inc(gathered[b], 16)

            def cut_traffic():
                sp.wait_ge(cut_flag, 1)
                sp.wait_ge(pos_ready, 1)
                with sp.Fori(0, NG) as g:
                    m = sp.value_load(cuti[0:1, bass.ds(g + NT, 1)], min_val=0, max_val=N)
                    with sp.If(m > KEEP):
                        with sp.Fori(0, NT // NG) as r:
                            t = g * (NT // NG) + r
                            n = sp.value_load(cuti[0:1, bass.ds(t, 1)], min_val=0, max_val=N)
                            with sp.If(n > KEEP):
                                sp.dma_start(cut_rows, adj[bass.ds(t * P, P), :]).then_inc(cut_loaded, 16)
                            with sp.Else():
                                sp.sem_inc(cut_loaded, 16)
                            wait_apart(sp, (cut_put, t + 1))
                    with sp.Else():
                        sp.sem_inc(cut_loaded, 16 * NT // NG)
                    wait_apart(sp, (cut_put, g * (NT // NG) + NT // NG))

            for L in layers:
                pack_traffic(L)
                expert_traffic(L)
                results_traffic(L)
            for b in range(NF):
                sp.wait_ge(combined, NF + b + 1)
                sp.dma_start(out[b * 4 * P:(b + 1) * 4 * P, :].rearrange("(t p) c -> p t c", p=P),
                             X[:, 4 * b:4 * b + 4, :]).then_inc(out_written, 16)
            sp.wait_ge(out_written, 16 * NF)

        @block.gpsimd
        def _(pool):
            step = Steps(pool, pool_steps)
            pool.sem_inc(xn_ready, 2)
            for m in (ident, identb, identh, before):
                step(pool.memset(m[:, :], 0.0))
            step(pool.memset(ones[:, :], 1.0))
            step(pool.memset(zero1[:, :], 0.0))
            for m in (ident, identb, identh):
                step(pool.affine_select(out=m[:, :], in_=m[:, :], compare_op=ALU.not_equal, fill=1.0, base=0,
                                        pattern=[[-1, P]], channel_multiplier=1))
            step(pool.affine_select(out=before[:, :], in_=before[:, :], compare_op=ALU.is_ge, fill=1.0, base=0,
                                    pattern=[[-1, P]], channel_multiplier=1))
            step(pool.iota(iotas[:, 0:E1], [[1, E1]], base=0, channel_multiplier=0))
            step(pool.iota(iotas[:, E1:E1 + NT], [[P, NT]], base=0, channel_multiplier=0))
            step(pool.iota(iotas[:, E1 + NT:E1 + NT + 1], [[1, 1]], base=0, channel_multiplier=1))
            step(pool.iota(tokens[:, :], [[P, NT]], base=0, channel_multiplier=1))
            step(pool.tensor_copy(iotaE[:, :], iotas[:, 0:E1]))
            step(pool.tensor_copy(step128[:, :], iotas[:, E1:E1 + NT]))
            pool.tensor_copy(iotaP[:, :], iotas[:, E1 + NT:E1 + NT + 1]).then_inc(constants_ready, 1)

            pool.wait_ge(deg_ready, 1)
            step(pool.partition_all_reduce(degmax[:, :], degx[:, :], P, bass.bass_isa.ReduceOp.max))
            pool.tensor_copy(cuti[0:1, :], degmax[0:1, :]).then_inc(cut_flag, 1)

            step(pool.memset(blank, 0.0))
            step(pool.iota(blank[:, :, D].bitcast(i32), [[P, RING]], base=2 * N, channel_multiplier=1))
            pool.sem_inc(rows_cleared, 1)

            def pack(L):
                nb, n = L["nb"], L["n"]
                base = pool_steps_n[0]
                with pool.Fori(0, L["E"] // nb) as i:
                    for b in range(nb):
                        e = i * nb + b
                        high, low = packed(L, b)
                        if n:
                            wait_apart(pool, (pack_scaled, e + 1))
                            pool.tensor_tensor(low, L["pack32"][:, b, :], high, ALU.subtract).then_inc(pack_done, 1)
                            continue
                        wait_apart(pool, (pack_in[n][b], i * 32 + 32), (pack_out[n][b], i * 16 + 16))
                        pool.tensor_scalar(L["pack32"][:, b, :], L["pack32"][:, b, :], WSCALE, None, ALU.mult) \
                            .then_inc(pool_steps, 1)
                        wait_apart(pool, (pool_steps, e * 2 + (base + 1)))
                        pool.tensor_copy(high, L["pack32"][:, b, :]).then_inc(pool_steps, 1)
                        wait_apart(pool, (pool_steps, e * 2 + (base + 2)))
                        pool.tensor_tensor(low, L["pack32"][:, b, :], high, ALU.subtract).then_inc(pack_done, 1)
                pool_steps_n[0] = base + (0 if n else 2 * L["E"])

            def exchange(L):
                n, jb = L["n"], L["jb"]
                for i in range(NF):
                    pool.wait_ge(xn_copied, NF * n + i + 1)
                    pool.tensor_tensor(XN[:, 4 * i:4 * i + 4, D:2 * D], fours(L["four"])[0][:, i % 2, :]
                                       .rearrange("p (t c) -> p t c", c=D), XN[:, 4 * i:4 * i + 4, 0:D], ALU.subtract) \
                        .then_inc(xn_ready, 1)
                pool.wait_ge(xn_ready, 2 + NF * (1 + n))
                pool.wait_ge(prefilled, PREFILLS)
                step = Steps(pool, pool_steps)
                step.n = pool_steps_n[0]
                for k in range(2):
                    pool.wait_ge(slots_known, 2 * n + k + 1)
                    step(pool.tensor_scalar(XN_row, tokens[:, :], k * N, None, ALU.add))
                    for t in range(NT):
                        pool.indirect_dma_start(
                            out=slots_dram[n], out_offset=bass.IndirectOffsetOnAxis(ap=pos[:, k, t:t + 1], axis=0),
                            in_=XN[:, t, :], in_offset=None).then_inc(scattered, 16)
                    pool.wait_ge(scattered, 16 * NT * (2 * n + k + 1))
                pool_steps_n[0] = step.n

                def rows_out(i, g):
                    waits = [(tokens_in[g], i * 16 + (16 * (jb // RING) + 16))]
                    if not isinstance(i, int) or i or n:
                        waits.append((put_back[g], i * (16 * XG) + 16 * XG * (jb // RING)))
                    wait_apart(pool, *waits)
                    pool.tensor_copy(rows[:, g, :], xss_row[:, g, :]).then_inc(rows_copied, 1)
                    wait_apart(pool, (rows_copied, i * 2 + (2 * jb // RING + g + 1)))
                    for s in range(XG):
                        wait_apart(pool, (o_copied, i * RING + (g * XG + s + jb + 3)))
                        pool.indirect_dma_start(
                            out=results_dram, out_offset=bass.IndirectOffsetOnAxis(ap=rows[:, g, s:s + 1], axis=0),
                            in_=yss[:, g, s, :], in_offset=None).then_inc(put_back[g], 16)

                for g in range(2):
                    rows_out(0, g)
                with pool.Fori(1, L["tiles"] // RING) as i:
                    for g in range(2):
                        rows_out(i, g)

            pool_steps_n = [step.n]
            pack(layers[0])
            exchange(layers[0])
            pack(layers[1])
            exchange(layers[1])

        @block.scalar
        def _(act):
            def cast(gg, u, deep):
                for j in range(GRP):
                    for s in range(4):
                        free = [(chunk_done, gg * (2 * NCH) + (u + 1) * NCH)] if j + s == 0 else []
                        kind = j if deep else 0
                        loads = gg * 32 + 16 * (u + 1) if deep else gg * 64 + 16 * (2 * u + j + 1 - DEEP // 2)
                        wait_apart(act, *free, (arrived[kind][s], loads))
                        nc.scalar.activation(nat[:, u, j, s * 1024:(s + 1) * 1024], stage[kind][:, s, :], ACT.Copy,
                                             accum_out=dpart[:, u, j, s:s + 1], saturate=False).then_inc(cast_done, 1)

            roots = [0]

            def root():
                roots[0] += 1
                act.wait_ge(root_in, roots[0])
                nc.scalar.activation(small[:, 1, :], small[:, 0, :], ACT.Sqrt).then_inc(root_out, 1)

            cast(0, 0, True)
            root()
            cast(0, 1, True)
            with act.Fori(1, DEEP // (2 * GRP)) as gg:
                cast(gg, 0, True)
                cast(gg, 1, True)
            with act.Fori(DEEP // (2 * GRP), NT // (2 * GRP)) as gg:
                cast(gg, 0, False)
                cast(gg, 1, False)
            root()
            root()
            for b in range(4):
                e = slice(8 * b, 8 * b + 8)
                act.wait_ge(z_scaled, b + 1)
                nc.scalar.activation(Z[:, e, 0:D], msum[:, e, 0:D], ACT.Copy).then_inc(z_high, 1)

            def scale_experts(h, u):
                L = layers[1]
                for b in (2 * u, 2 * u + 1):
                    high, _ = packed(L, b)
                    wait_apart(act, (pack_in[1][b], h * 32 + 32), (pack_out[1][b], h * 16 + 16))
                    nc.scalar.activation(high, L["pack32"][:, b, :], ACT.Copy, scale=WSCALE)
                    nc.scalar.activation(L["pack32"][:, b, :], L["pack32"][:, b, :], ACT.Copy, scale=WSCALE) \
                      .then_inc(pack_scaled, 1)

            def low_parts(r, scale):
                with act.Fori(0, NT // 2) as h:
                    for u in range(2):
                        act.wait_ge(y_done, h * 2 + (r * NT + u + 1))
                        act.wait_ge(y_free, h * 2 + (r * NT + u + 1))
                        nc.scalar.activation(ylow[:, u, :], psY[u][:, D:2 * D], ACT.Copy,
                                             scale=scale(h * 2 + u)).then_inc(y_low, 1)
                        if r:
                            scale_experts(h, u)

            def transposes_out(p, keep=False, hidden=False):
                four, fourT, h2T = fours(p["four"])
                with act.Fori(0, NF // 2) as h:
                    for u in range(2):
                        i = h * 2 + u
                        act.wait_ge(four_T, i + (NF * p["q"] + 1))
                        act.wait_ge(four_mm, i + (NF * p["q"] + 1))
                        nc.scalar.activation(fourT[:, u, :], psC[u], ACT.Copy).then_inc(four_Tc, 1)
                        if keep:
                            nc.scalar.activation(XN[:, bass.ds(i * 4, 4), 0:D], four[:, u, :].rearrange("p (t c) -> p t c", c=D),
                                                 ACT.Copy).then_inc(xn_copied, 1)
                        if hidden:
                            act.wait_ge(h2_done, i + 1)
                            nc.scalar.activation(h2T[:, u, :], psH2[u], ACT.Tanh, bias=bproj_s[:, :]) \
                              .then_inc(h2_act, 1)

            def experts(L):
                act.wait_ge(gate_in, 1 + L["n"])
                nc.scalar.activation(gsmall[:, 1, :], gsmall[:, 0, :], ACT.Exp).then_inc(gate_exp, 1)
                act.wait_ge(eid_ready, 1 + L["n"])

                def expert_of(j):
                    return act.value_load(eid[0:1, bass.ds(j, 1)], min_val=0, max_val=L["E"] - 1)

                def hidden(s, j, e):
                    act.wait_ge(h_done, j + (L["jb"] + 3))
                    for h in range(2):
                        last = nc.scalar.activation(psH[s % 4][:, h, :], psH[s % 4][:, h, :], ACT.Relu,
                                                    scale=1.0 / WSCALE, bias=L["b1T"][:, h, bass.ds(e, 1)])
                    last.then_inc(relu_done, 1)
                    if s + 1 < RING:
                        e = expert_of(j + 1)
                    act.wait_ge(relu_done, j + (L["jb"] + 1))
                    act.wait_ge(o_done, j + (L["jb"] + 1))
                    nc.scalar.activation(hTs[:, s % 4, 0, :, :], psH[s % 4], ACT.Copy).then_inc(h_act, 1)
                    return e

                def load_tokens(g, j):
                    act.dma_start(xss[:, g, :, :], slots_dram[L["n"]][bass.ds(j * P, XG * P), :].rearrange("(s p) c -> p s c", p=P)) \
                      .then_inc(tokens_in[g], 16)

                act.wait_ge(pos_ready, 1 + L["n"])
                act.wait_ge(cut_put, NT)
                for b in range(L["nb"]):
                    act.wait_ge(pack_out[L["n"]][b], 16 + 16 * (L["E"] // L["nb"]))
                act.wait_ge(scattered, 16 * 2 * NT * (1 + L["n"]))
                for g in range(2):
                    load_tokens(g, g * XG)
                with act.Fori(0, L["tiles"] // RING - 1) as i:
                    e = expert_of(i * RING)
                    for s in range(RING):
                        e = hidden(s, i * RING + s, e)
                        if s % XG == XG - 2:
                            wait_apart(act, (rows_copied, i * 2 + (2 * L["jb"] // RING + s // XG + 1)))
                            load_tokens(s // XG, i * RING + (RING + s - XG + 2))
                j = L["tiles"] - RING
                e = expert_of(j)
                for s in range(RING):
                    e = hidden(s, j + s, e)

            low_parts(0, lambda t: rsd[:, bass.ds(t, 1)])
            transposes_out(mix)
            root()
            act.wait_ge(pack_out[0][0], 16 + 16 * E0)
            act.wait_ge(prefilled, PREFILLS)
            transposes_out(layers[0], keep=True)
            experts(layers[0])
            root()
            act.wait_ge(constants_ready, 1)
            nc.scalar.activation(tanh1[:, :], ones[:, 0:1], ACT.Tanh).then_inc(tanh_ready, 1)
            transposes_out(proj, hidden=True)
            low_parts(1, lambda t: 1.0)
            root()
            transposes_out(layers[1], keep=True)
            experts(layers[1])

        @block.vector
        def _(dve):
            v = nc.vector
            step = Steps(dve, dve_steps)
            dve.sem_inc(chunk_free, NCH)
            dve.sem_inc(words_free, 2)
            dve.sem_inc(y_free, 2)
            dve.sem_inc(four_free, 2)
            dve.sem_inc(o_copied, 2)
            roots = [0]

            def inverse_root(dst, src_op, scale):
                roots[0] += 1
                src_op(small[:, 0, :]).then_inc(root_in, 1)
                dve.wait_ge(root_in, roots[0])
                dve.wait_ge(root_out, roots[0])
                step(v.reciprocal(small[:, 2, :], small[:, 1, :]))
                step(v.tensor_tensor(small[:, 2, :], small[:, 2, :], small[:, 0, :], ALU.mult))
                step(v.tensor_tensor(small[:, 2, :], small[:, 2, :], small[:, 1, :], ALU.add))
                step(v.reciprocal(small[:, 3, :], small[:, 2, :]))
                step(v.tensor_scalar(dst[:, :], small[:, 3, :], 2.0 * scale, None, ALU.mult))

            def norm_stats():
                a, b, c = small[:, 1, :], small[:, 2, :], small[:, 3, :]
                step(v.tensor_tensor(a, stats[:, :, 1], stats[:, :, 4], ALU.add))
                step(v.tensor_scalar(mean[:, :], a, 0.5, None, ALU.mult))
                step(v.tensor_tensor(b, stats[:, :, 1], stats[:, :, 4], ALU.subtract))
                step(v.tensor_tensor(b, b, b, ALU.mult))
                step(v.tensor_tensor(c, stats[:, :, 2], stats[:, :, 5], ALU.add))
                step(v.scalar_tensor_tensor(c, b, D / 4.0, c, ALU.mult, ALU.add))
                inverse_root(rstd, lambda o: v.tensor_scalar(o, c, 1.0 / D, EPS, ALU.mult, ALU.add), 1.0)

            step(v.memset(big1[:, :], 0.0))
            step(v.memset(xr[:, :, :, 0, D + 1:MW], 1.0))
            step(v.memset(xr[:, :, :, 1, D + 1:MW], 0.0))
            dve.wait_ge(x_loaded, 16)
            with dve.Fori(0, NF) as i:
                for j in range(4):
                    last = v.bn_stats(stats[:, bass.ds(i * 4 + j, 1), :].rearrange("p t c -> p (t c)"),
                                      X[:, bass.ds(i * 4 + j, 1), :].rearrange("p t c -> p (t c)"))
                last.then_inc(dve_steps, 1)
            step.n += NF
            dve.wait_ge(dve_steps, step.n)
            norm_stats()
            step(v.tensor_scalar(rstd01[:, :], rstd[:, :], 0.1, None, ALU.mult))
            dve.wait_ge(setup_T, 1)
            dve.wait_ge(constants_ready, 1)
            step(v.scalar_tensor_tensor(wmix[:, :], PS[:, 2, 0:D], 1.0, ident[:, :], ALU.mult, ALU.add))
            step(v.tensor_scalar(wmix[:, :], wmix[:, :], 0.5, None, ALU.mult))
            step(v.tensor_copy(b1T1[:, :, :], PS[:, 3, 0:2 * E1].rearrange("p (h e) -> p h e", h=2)))
            step(v.tensor_tensor(rb0[:, 0, :], rb0[:, 0, :], rb0[:, 1, :], ALU.add))
            v.tensor_copy(b1T0[:, :, :], PS[:, 4, 0:2 * E0].rearrange("p (h e) -> p h e", h=2)).then_inc(setup_used, 1)
            dve.wait_ge(setup_used, 1)

            def chained(ins, n):
                ins.then_inc(dve_steps, 1)
                wait_apart(dve, (dve_steps, n))

            def tokens_of(g, u, chain):
                for j in range(GRP):
                    chained(v.tensor_scalar(xf[:, j, :], X[:, bass.ds(g * GRP + j, 1), :].rearrange("p t c -> p (t c)"),
                                            mean[:, bass.ds(g * GRP + j, 1)], rstd[:, bass.ds(g * GRP + j, 1)],
                                            ALU.subtract, ALU.mult), chain + (j + 1))
                wait_apart(dve, (chunk_done, g * NCH + NCH))
                chained(v.tensor_copy(xr[:, u, :, 0, 0:D], xf[:, :, :]), chain + 3)
                v.tensor_tensor(xr[:, u, :, 1, 0:D], xf[:, :, :], xr[:, u, :, 0, 0:D], ALU.subtract)

            def degrees_of(g, u, chain):
                wait_apart(dve, (cast_done, g * (4 * GRP) + 4 * GRP))
                chained(v.reduce_sum(deg[:, bass.ds(g * GRP, GRP)], dpart[:, u, :, :], AX.X), chain + 4)
                chained(v.tensor_copy(xr[:, u, :, 0, D:D + 1].rearrange("p j c -> p (j c)"), deg[:, bass.ds(g * GRP, GRP)]),
                        chain + 5)
                v.tensor_tensor(xr[:, u, :, 1, D:D + 1].rearrange("p j c -> p (j c)"), deg[:, bass.ds(g * GRP, GRP)],
                                xr[:, u, :, 0, D:D + 1].rearrange("p j c -> p (j c)"), ALU.subtract).then_inc(xr_ready, 1)

            def group(gg, u, chain, last=False):
                g = gg * 2 + u

                def words(w):
                    wait_apart(dve, (words_T, g * 4 + w + 1))
                    v.tensor_copy(adjT[:, bass.ds(g * GRP + w // 2, 1), (w % 2) * 1024:(w % 2 + 1) * 1024]
                                  .rearrange("p t w -> p (t w)"),
                                  PS[:, w % 2, :].bitcast(u16)).then_inc(words_free, 1)

                def sums(c):
                    n = min(CH, 2 * NK - CH * c)
                    dve.wait_ge(chunk_done, g * NCH + (2 * NCH + c + 1))
                    dve.wait_ge(chunk_free, g * NCH + c + 1)
                    v.tensor_tensor(msum[:, CH * c:CH * c + n, :], psM[c % 6][:, 0:n, :],
                                    msum[:, CH * c:CH * c + n, :], ALU.add).then_inc(chunk_free, 1)

                for kind, i in ORDER:
                    (words if kind == "T" else sums)(i)
                    if (kind, i) == ("C", 5) and not last:
                        tokens_of(g + 1, 1 - u, chain)
                    if (kind, i) == ("C", NCH - 2) and not last:
                        degrees_of(g + 1, 1 - u, chain)

            base = step.n + 5
            tokens_of(0, 0, step.n)
            degrees_of(0, 0, step.n)
            final = NT // (2 * GRP) - 1
            with dve.Fori(0, final) as gg:
                group(gg, 0, gg * 10 + base)
                group(gg, 1, gg * 10 + (base + 5))
            group(final, 0, final * 10 + base)
            group(final, 1, final * 10 + (base + 5), last=True)
            step.n = base + final * 10 + 5
            dve.wait_ge(chunk_free, NCH * (NT // GRP) + NCH)
            dve.wait_ge(xr_ready, NT // GRP)
            v.reduce_max(degx[:, NT:NT + NG], deg.rearrange("p (g t) -> p g t", g=NG), AX.X).then_inc(deg_ready, 1)

            inverse_root(rsd, lambda o: v.tensor_copy(o, deg[:, :]), 0.9)
            step(v.reciprocal(small[:, 2, :], msum[:, :, D + 1]))
            inverse_root(redge, lambda o: v.tensor_tensor(o, msum[:, :, D], small[:, 2, :], ALU.mult), 1.0)
            for b in range(4):
                e = slice(8 * b, 8 * b + 8)
                v.tensor_tensor(msum[:, e, 0:D], msum[:, e, 0:D],
                                redge[:, e].unsqueeze(2).to_broadcast((P, 8, D)), ALU.mult).then_inc(z_scaled, 1)
            for b in range(4):
                e = slice(8 * b, 8 * b + 8)
                dve.wait_ge(z_scaled, b + 1)
                dve.wait_ge(z_high, b + 1)
                v.tensor_tensor(Z[:, e, D:2 * D], msum[:, e, 0:D], Z[:, e, 0:D], ALU.subtract).then_inc(z_ready, 1)
            dve.wait_ge(z_ready, 4)

            def product(r, post, k):
                def copy_block(t, u):
                    v.tensor_copy(block_words[:, u, :], adjT[:, bass.ds(t, 1), :].rearrange("p t w -> p (t w)")) \
                     .then_inc(blk_ready, 1)

                def after(t, u, n):
                    dve.wait_ge(y_done, t + (r * NT + 1))
                    dve.wait_ge(y_low, t + (r * NT + 1))
                    post(t, u, n)

                base = step.n
                copy_block(0, 0)
                copy_block(1, 1)
                with dve.Fori(0, NT // 2 - 1) as h:
                    for u in range(2):
                        after(h * 2 + u, u, h * (2 * k) + (base + u * k))
                        copy_block(h * 2 + u + 2, u)
                for u in range(2):
                    after(NT - 2 + u, u, base + (NT - 2 + u) * k)
                step.n = base + NT * k

            def tile_of(a, t):
                return a[:, bass.ds(t, 1), :].rearrange("p t c -> p (t c)")

            def mixed(t, u, n):
                step.n = n
                v.scalar_tensor_tensor(ysum[:, u, :], psY[u][:, 0:D], rsd[:, bass.ds(t, 1)], ylow[:, u, :],
                                       ALU.mult, ALU.add).then_inc(y_free, 1)
                step(v.tensor_scalar(tile_of(comb, t), tile_of(X, t), mean[:, bass.ds(t, 1)], rstd01[:, bass.ds(t, 1)],
                                     ALU.subtract, ALU.mult))
                step(v.tensor_tensor(tile_of(comb, t), tile_of(comb, t), ysum[:, u, :], ALU.add))

            product(0, mixed, 2)

            def pass_fours(p, fill, use):
                def use_i(i, u):
                    dve.wait_ge(four_mm, i + (NF * p["q"] + 3))
                    use(i, u)

                fill_ahead(dve, fill, use_i)

            four, fourT, h2T = fours(big3)

            def fill_mix(i, u):
                v.tensor_copy(four[:, u, :], comb[:, bass.ds(i * 4, 4), :].rearrange("p t c -> p (t c)")) \
                 .then_inc(four_ready, 1)

            def use_mix(i, u):
                flat = X[:, bass.ds(i * 4, 4), :].rearrange("p t c -> p (t c)")
                v.tensor_tensor(flat, flat, psR[u], ALU.add).then_inc(four_free, 1)
                dve.wait_ge(four_free, i + 3)
                for j in range(4):
                    last = v.bn_stats(stats[:, bass.ds(i * 4 + j, 1), :].rearrange("p t c -> p (t c)"),
                                      tile_of(X, i * 4 + j))
                last.then_inc(dve_steps, 1)

            def fill_norm(p):
                four, _, _ = fours(p["four"])

                def fill(i, u):
                    if "n" in p:
                        dve.wait_ge(xn_ready, i + (NF * p["n"] + 1))
                    for j in range(4):
                        last = v.tensor_scalar(four[:, u, j * D:(j + 1) * D], tile_of(X, i * 4 + j),
                                               mean[:, bass.ds(i * 4 + j, 1)], rstd[:, bass.ds(i * 4 + j, 1)],
                                               ALU.subtract, ALU.mult)
                    last.then_inc(four_ready, 1)
                return fill

            pass_fours(mix, fill_mix, use_mix)
            step.n += NF
            dve.wait_ge(dve_steps, step.n)
            norm_stats()

            def use_router(L):
                E = L["E"]
                four, _, _ = fours(L["four"])
                bias = rb0[:, 0, :] if L["n"] == 0 else rb1[:, :]
                base = step.n

                def use(i, u):
                    step.n = i * 3 + base
                    dve.wait_ge(dve_steps, step.n)
                    l3 = l4[:, :, 0:E]
                    v.tensor_tensor(l3, psR[u][:, 0:4 * E].rearrange("p (t e) -> p t e", t=4),
                                    bias.unsqueeze(1).to_broadcast((P, 4, E)), ALU.add).then_inc(four_free, 1)
                    wait_apart(dve, (four_free, i + (NF * L["q"] + 3)))
                    for j in range(4):
                        last = v.max(out=top[:, j, :], in_=l4[:, j, 0:E])
                    step(last, alone=True)
                    for j in range(4):
                        last = v.max_index(topi[:, j, :], top[:, j, :], l4[:, j, 0:E])
                    step(last, alone=True)
                    v.tensor_copy(val12[:, bass.ds(i * 4, 4), :], top[:, :, 0:2])
                    step(v.tensor_copy(idx12[:, bass.ds(i * 4, 4), :], topi[:, :, 0:2]))
                pass_fours(L, fill_norm(L), use)
                step.n = base + 3 * NF

            def route(L):
                E, n, part = L["E"], L["n"], L["part"]
                et = lambda a: a.rearrange("p (e t) -> p e t", t=NT)
                over_t = lambda a: a.unsqueeze(2).to_broadcast((P, E, NT))
                over_e = lambda a: a.unsqueeze(1).to_broadcast((P, E, NT))
                for k in range(2):
                    step(v.tensor_tensor(et(L["oh"][k]), over_t(iotaE[:, 0:E]), over_e(idx12[:, :, k]), ALU.is_equal))
                v.tensor_tensor(L["both"], L["oh"][0], L["oh"][1], ALU.add).then_inc(cnt_ready, 1)
                v.tensor_tensor(gsmall[:, 0, :], val12[:, :, 1], val12[:, :, 0], ALU.subtract).then_inc(gate_in, 1)
                dve.wait_ge(cnt_done, 1 + n)
                w = E * NT
                tot, rank = banks[:, 0:w], banks[:, 2048:2048 + w]
                run, excl, a, b = part[3], part[4], part[5], part[6]
                step(v.tensor_tensor_scan(run, zero1[:, :].to_broadcast((P, w)), tot, 0.0, ALU.add, ALU.add))
                step(v.tensor_tensor(excl, run, tot, ALU.subtract))
                count, tiles, upto, begin, shift = (expt[:, i, 0:E] for i in range(5))
                first = et(excl)[:, :, 0]
                step(v.tensor_tensor(count, et(run)[:, :, NT - 1], first, ALU.subtract))
                step(v.tensor_tensor(et(a), over_t(count), over_e(step128[:, :]), ALU.is_gt))
                step(v.reduce_sum(tiles, et(a), AX.X))
                step(v.tensor_tensor_scan(upto, zero1[:, :].to_broadcast((P, E)), tiles, 0.0, ALU.add, ALU.add))
                step(v.tensor_tensor(begin, upto, tiles, ALU.subtract))
                step(v.scalar_tensor_tensor(shift, begin, float(P), first, ALU.mult, ALU.subtract))
                step(v.tensor_tensor(et(a), et(excl), over_t(shift), ALU.add))
                step(v.tensor_tensor(a, a, rank, ALU.add))
                for k in range(2):
                    step(v.tensor_tensor(b, L["oh"][k], a, ALU.mult))
                    step(v.reduce_sum(posf[:, k, :], b.rearrange("p (e t) -> p t e", t=NT), AX.X))
                    v.tensor_copy(pos[:, k, :], posf[:, k, :]).then_inc(slots_known, 1)
                    if k == 0:
                        step(v.tensor_tensor(part[2][:, 0:E], upto, iotaP[:, :].to_broadcast((P, E)), ALU.is_le))
                        step(v.reduce_sum(eidc[:, :], part[2][:, 0:E], AX.X))
                        v.tensor_scalar(eidc[:, :], eidc[:, :], float(E - 1), None, ALU.min).then_inc(eid_col, 1)
                dve.wait_ge(eid_row, 1 + n)
                v.tensor_copy(eid[:, :], PS[0:1, 0, 0:P]).then_inc(eid_ready, 1)
                dve.wait_ge(eid_ready, 1 + n)
                dve.sem_inc(pos_ready, 1)
                dve.wait_ge(gate_exp, 1 + n)
                step(v.tensor_scalar(gsmall[:, 0, :], gsmall[:, 1, :], 1.0, None, ALU.add))
                step(v.reciprocal(gate[:, 0, :], gsmall[:, 0, :]))
                step(v.tensor_tensor(gate[:, 1, :], gate[:, 0, :], gsmall[:, 1, :], ALU.mult))

            def expert_loop(L):
                jb = L["jb"]
                dve.wait_ge(b2_loaded, 16 * (1 + L["n"]))
                dve.wait_ge(eid_ready, 1 + L["n"])

                def turned(s, j):
                    wait_apart(dve, (xT_done, j + (jb + 1)), (h_done, j + (jb + 1)))
                    v.tensor_copy(xTs[:, s % 2, :, :], psX[s % 2]).then_inc(xT_copied, 1)

                def low(s, j):
                    dve.wait_ge(h_act, j + (jb + 1))
                    v.tensor_tensor(hTs[:, s % 4, 1, :, :], psH[s % 4], hTs[:, s % 4, 0, :, :], ALU.subtract) \
                     .then_inc(split_low, 1)

                def expert_of(j):
                    return dve.value_load(eid[0:1, bass.ds(j, 1)], min_val=0, max_val=L["E"] - 1)

                def result(i, s, j, e):
                    dve.wait_ge(o_done, j + (jb + 5))
                    if s % XG == 0 and (not isinstance(i, int) or i or L["n"]):
                        dve.wait_ge(put_back[s // XG], i * (16 * XG) + 16 * XG * (jb // RING))
                    v.scalar_tensor_tensor(yss[:, s // XG, s % XG, :], psO[s % 2], 1.0 / WSCALE, L["b2s"][:, bass.ds(e * D, D)],
                                           ALU.mult, ALU.add) \
                     .then_inc(o_copied, 1)

                turned(0, 0)

                def body(i, s, j):
                    if not isinstance(j, int) or j + 1 < L["tiles"]:
                        turned((s + 1) % RING, j + 1)
                    if not isinstance(j, int) or j >= 2:
                        e = expert_of(j - 2)
                    if not isinstance(j, int) or j >= 1:
                        low((s - 1) % RING, j - 1)
                    if not isinstance(j, int) or j >= 2:
                        result(i if s >= 2 else i - 1, (s - 2) % RING, j - 2, e)
                ring_rounds(dve, L["tiles"], body)
                low(RING - 1, L["tiles"] - 1)
                for s in (RING - 2, RING - 1):
                    j = L["tiles"] - RING + s
                    result(L["tiles"] // RING - 1, s, j, expert_of(j))

            def combine(L):
                n = L["n"]
                for b in range(NF):
                    t = slice(4 * b, 4 * b + 4)
                    dve.wait_ge(gathered[b], 32 * (n + 1))
                    for k in range(2):
                        for tt in range(4 * b, 4 * b + 4):
                            last = v.scalar_tensor_tensor(X[:, tt, :], gath[k][:, tt, :], gate[:, k, tt:tt + 1], X[:, tt, :],
                                                          ALU.mult, ALU.add)
                        if k == 0:
                            step(last)
                    last.then_inc(combined, 1)
                    if n == 0:
                        dve.wait_ge(combined, b + 1)
                        for tt in range(4 * b, 4 * b + 4):
                            last = v.bn_stats(stats[:, tt, :], X[:, tt, :])
                        step(last)

            def cut():
                base, S = step.n, 4
                dve.wait_ge(cut_flag, 1)
                dve.wait_ge(pos_ready, 1)

                def tile(t):
                    n = dve.value_load(cuti[0:1, bass.ds(t, 1)], min_val=0, max_val=N)
                    wait_apart(dve, (cut_loaded, t * 16 + 16))
                    with dve.If(n > KEEP):
                        taken = [0]

                        def chained(ins):
                            taken[0] += 1
                            ins.then_inc(dve_steps, 1)
                            wait_apart(dve, (dve_steps, t * S + (base + taken[0])))

                        def count(h):
                            half = slice(h * N // 2, (h + 1) * N // 2)
                            return v.tensor_tensor_scan(cut_count, zero1[:, :].to_broadcast((P, N // 2)), cut_rows[:, half],
                                                        carry[:, :] if h else 0.0, ALU.add, ALU.add)

                        def mask(h):
                            half = slice(h * N // 2, (h + 1) * N // 2)
                            return v.scalar_tensor_tensor(cut_nat[:, half], cut_count, float(KEEP), cut_rows[:, half],
                                                          ALU.is_le, ALU.mult, saturate=False)

                        chained(count(0))
                        v.tensor_copy(carry[:, :], cut_count[:, N // 2 - 1:N // 2]).then_inc(dve_steps, 1)
                        mask(0).then_inc(dve_steps, 1)
                        wait_apart(dve, (dve_steps, t * S + (base + 3)))
                        taken[0] += 2
                        chained(count(1))
                        mask(1).then_inc(cut_masked, 1)
                    with dve.Else():
                        dve.sem_inc(dve_steps, S)
                        dve.sem_inc(cut_masked, 1)
                    wait_apart(dve, (cut_T, t + 1))
                    with dve.If(n > KEEP):
                        for w in range(2):
                            last = v.tensor_copy(adjT[:, bass.ds(t, 1), w * 1024:(w + 1) * 1024].rearrange("p t w -> p (t w)"),
                                                 PS[:, w, :].bitcast(u16))
                        last.then_inc(cut_put, 1)
                    with dve.Else():
                        dve.sem_inc(cut_put, 1)

                R = NT // NG
                with dve.Fori(0, NG) as g:
                    m = dve.value_load(cuti[0:1, bass.ds(g + NT, 1)], min_val=0, max_val=N)
                    with dve.If(m > KEEP):
                        with dve.Fori(0, R) as r:
                            tile(g * R + r)
                    with dve.Else():
                        wait_apart(dve, (cut_loaded, g * (16 * R) + 16 * R))
                        dve.sem_inc(dve_steps, S * R)
                        dve.sem_inc(cut_masked, R)
                        wait_apart(dve, (cut_T, g * R + R))
                        dve.sem_inc(cut_put, R)
                step.n = base + S * NT
                dve.wait_ge(cut_put, NT)

            use_router(layers[0])
            route(layers[0])
            cut()
            expert_loop(layers[0])
            combine(layers[0])
            norm_stats()

            dve.wait_ge(tanh_ready, 1)

            def use_proj(i, u):
                e4 = Z[:, bass.ds(i * 4, 4), 0:D]
                l4_ = Z[:, bass.ds(i * 4, 4), D:2 * D]
                src = psR[u].rearrange("p (e c) -> p e c", e=4)
                v.tensor_scalar(e4, src, tanh1[:, :], None, ALU.mult).then_inc(z_ready, 1)
                dve.wait_ge(z_ready, i + 5)
                v.scalar_tensor_tensor(l4_, src, tanh1[:, :], e4, ALU.mult, ALU.subtract).then_inc(four_free, 1)

            pass_fours(proj, fill_norm(proj), use_proj)
            dve.wait_ge(four_free, 2 + 3 * NF)

            def graph2(t, u, n):
                step.n = n
                v.tensor_tensor(ysum[:, u, :], psY[u][:, 0:D], ylow[:, u, :], ALU.add).then_inc(y_free, 1)
                dve.wait_ge(y_free, t + (NT + 3))
                step(v.tensor_tensor(ysum[:, u, :], ysum[:, u, :], bgcn_s[:, :], ALU.add))
                step(v.scalar_tensor_tensor(tile_of(X, t), ysum[:, u, :], 0.0, tile_of(X, t), ALU.max, ALU.add))
                step(v.bn_stats(stats[:, bass.ds(t, 1), :].rearrange("p t c -> p (t c)"), tile_of(X, t)))

            product(1, graph2, 3)
            norm_stats()
            use_router(layers[1])
            route(layers[1])
            expert_loop(layers[1])
            combine(layers[1])

        @block.tensor
        def _(pe):
            mm = nc.tensor.matmul
            pe.sem_inc(chunk_done, 2 * NCH)
            pe.sem_inc(four_mm, 2)
            pe.sem_inc(h_done, 2)
            pe.sem_inc(o_done, 4)
            pe.wait_ge(constants_ready, 1)
            pe.wait_ge(weights_loaded, 16 * 12)
            mm(PS[:, 2, 0:D], wnat, ident[:, :], start=True, stop=True)
            for h in range(2):
                mm(PS[:, 3, h * E1:(h + 1) * E1], b1n1[:, h * P:(h + 1) * P], ident[0:E1, 0:E1], start=True, stop=True)
            for h in range(2):
                last = mm(PS[:, 4, h * E0:(h + 1) * E0], b1n0[:, h * P:(h + 1) * P], ident[0:E0, 0:E0], start=True, stop=True)
            last.then_inc(setup_T, 1)
            pe.wait_ge(setup_used, 1)

            def turn_words(src, bank, half):
                words = src.bitcast(bf16)
                for k in range(8):
                    last = pe.transpose(psT[bank][:, k, :], words[:, (8 * half + k) * P:(8 * half + k + 1) * P], identb[:, :])
                return last

            def group(gg, u):
                g = gg * 2 + u
                pe.wait_ge(cast_done, g * (4 * GRP) + 4 * GRP)

                def words(w):
                    pe.wait_ge(words_free, g * 4 + w + 1)
                    turn_words(nat[:, u, w // 2, :], w % 2, w % 2).then_inc(words_T, 1)

                def sums(c):
                    n = min(CH, 2 * NK - CH * c)
                    wait_apart(pe, (chunk_free, g * NCH + (NCH + c - 5 if c >= 6 else c + 7 if c <= 4 else 6)),
                               (xr_ready, g + 1))
                    for e in range(n):
                        k, b = divmod(CH * c + e, 2)
                        for j in range(GRP):
                            a = nat[:, u, j, 256 * k + b:256 * (k + 1):2]
                            mm(psM[c % 6][:, e, :], a, xr[:, u, j, 0, :], start=(j == 0), stop=False)
                            last = mm(psM[c % 6][:, e, :], a, xr[:, u, j, 1, :], start=False, stop=(j == GRP - 1))
                    last.then_inc(chunk_done, 1)

                for kind, i in ORDER:
                    (words if kind == "T" else sums)(i)

            with pe.Fori(0, NT // (2 * GRP)) as gg:
                group(gg, 0)
                group(gg, 1)

            def product(r):
                with pe.Fori(0, NT // 2) as h:
                    for u in range(2):
                        t = h * 2 + u
                        wait_apart(pe, (blk_ready, t + (r * NT + 1)), (y_free, t + (r * NT + 1)))
                        for k in range(NK):
                            for b in range(2):
                                last = mm(psY[u], block8[:, u, k, :, b], Z[:, 2 * k + b, :],
                                          start=(k == 0 and b == 0), stop=(k == NK - 1 and b == 1))
                        last.then_inc(y_done, 1)

            def pass_fours(p, final):
                four, fourT, h2T = fours(p["four"])

                def turn(i, u):
                    pe.wait_ge(four_ready, i + (NF * p["q"] + 1))
                    for j in range(4):
                        last = pe.transpose(psC[u][:, j * P:(j + 1) * P], four[:, u, j * D:(j + 1) * D], ident[:, :])
                    last.then_inc(four_T, 1)

                def use(i, u):
                    pe.wait_ge(four_Tc, i + (NF * p["q"] + 1))
                    pe.wait_ge(four_free, i + (NF * p["q"] + 1))
                    final(i, u, fourT[:, u, :], h2T[:, u, :]).then_inc(four_mm, 1)

                with pe.Fori(0, NF // 2) as h:
                    for u in range(2):
                        turn(h * 2 + u, u)
                        use(h * 2 + u, u)

            def by_tile(w, n):
                def final(i, u, fT, hT):
                    for j in range(4):
                        last = mm(psR[u][:, j * n:(j + 1) * n], fT[:, j * P:(j + 1) * P], w, start=True, stop=True)
                    return last
                return final

            def projected(i, u, fT, hT):
                mm(psH2[u], wproj_s[:, :], fT, start=True, stop=True).then_inc(h2_done, 1)
                pe.wait_ge(h2_act, i + 1)
                for k in range(2):
                    for b in range(2):
                        q = 2 * k + b
                        last = mm(psR[u][:, q * D:(q + 1) * D], hT[:, 256 * k + b:256 * (k + 1):2], wgcn_s[:, :],
                                  start=True, stop=True)
                return last

            def cut():
                R = NT // NG
                pe.wait_ge(cut_flag, 1)
                with pe.Fori(0, NG) as g:
                    m = pe.value_load(cuti[0:1, bass.ds(g + NT, 1)], min_val=0, max_val=N)
                    with pe.If(m > KEEP):
                        with pe.Fori(0, R) as r:
                            t = g * R + r
                            n = pe.value_load(cuti[0:1, bass.ds(t, 1)], min_val=0, max_val=N)
                            pe.wait_ge(cut_masked, t + 1)
                            with pe.If(n > KEEP):
                                turn_words(cut_nat, 0, 0)
                                turn_words(cut_nat, 1, 1).then_inc(cut_T, 1)
                            with pe.Else():
                                pe.sem_inc(cut_T, 1)
                    with pe.Else():
                        pe.wait_ge(cut_masked, g * R + R)
                        pe.sem_inc(cut_T, R)

            def experts(L):
                E, jb = L["E"], L["jb"]
                w = E * NT
                pe.wait_ge(cnt_ready, 1 + L["n"])
                for m, at in ((ones, 0), (before, 2048)):
                    for c in range(0, w, 512):
                        n = min(512, w)
                        last = mm(banks[:, at + c:at + c + n], m[:, :], L["both"][:, c:c + n], start=True, stop=True)
                last.then_inc(cnt_done, 1)
                pe.wait_ge(eid_col, 1 + L["n"])
                mm(PS[0:1, 0, 0:P], eidc[:, :], ident[:, :], start=True, stop=True).then_inc(eid_row, 1)
                pe.wait_ge(pos_ready, 1 + L["n"])

                if L["n"] == 0:
                    cut()

                def turn(i, s, j):
                    if s % XG == 0:
                        wait_apart(pe, (tokens_in[s // XG], i * 16 + (16 * (jb // RING) + 16)))
                    for q in range(2):
                        last = pe.transpose(psX[s % 2][:, q, :], xss[:, s // XG, s % XG, q * D:(q + 1) * D], identh[:, :])
                    last.then_inc(xT_done, 1)

                def split(out, a, b):
                    mm(out, a[0], b[0], start=a[2], stop=False)
                    mm(out, a[0], b[1], start=False, stop=False)
                    return mm(out, a[1], b[0], start=False, stop=a[3])

                def hidden(i, s, j):
                    pe.wait_ge(weights_in[s], i * 16 + (16 * (jb // RING) + 16))
                    pe.wait_ge(xT_copied, j + (jb + 1))
                    for h in range(2):
                        hi, lo = (w1s[:, s, q, h * P:(h + 1) * P] for q in (0, 1))
                        last = split(psH[s % 4][:, h, :], (hi, lo, True, True), (xTs[:, s % 2, 0, :], xTs[:, s % 2, 1, :]))
                    last.then_inc(h_done, 1)

                def result(s, j):
                    pe.wait_ge(split_low, j + (jb + 1))
                    pe.wait_ge(o_copied, j + (jb + 1))
                    for h in range(2):
                        hi, lo = (hTs[:, s % 4, q, h, :] for q in (0, 1))
                        whi, wlo = (w2s[:, s, q, h * D:(h + 1) * D] for q in (0, 1))
                        last = split(psO[s % 2], (hi, lo, h == 0, h == 1), (whi, wlo))
                    last.then_inc(o_done, 1)

                turn(0, 0, 0)

                def body(i, s, j):
                    if not isinstance(j, int) or j + 1 < L["tiles"]:
                        turn(i if s + 1 < RING else i + 1, (s + 1) % RING, j + 1)
                    hidden(i, s, j)
                    if not isinstance(j, int) or j >= 2:
                        result((s - 2) % RING, j - 2)
                ring_rounds(pe, L["tiles"], body)
                for s in (RING - 2, RING - 1):
                    result(s, L["tiles"] - RING + s)

            pe.wait_ge(z_ready, 4)
            product(0)
            pass_fours(mix, by_tile(wmix[:, :], D))
            pass_fours(layers[0], by_tile(wr0_s[:, :], E0))
            experts(layers[0])
            pass_fours(proj, projected)
            pe.wait_ge(z_ready, 4 + NF)
            product(1)
            pass_fours(layers[1], by_tile(wr1_s[:, :], E1))
            experts(layers[1])


_INS = ['x', 'adj', 'L0_gnn_W', 'L0_ffn_Wg', 'L0_ffn_bg', 'L0_ffn_bias', 'L0_ffn_W1', 'L0_ffn_b1', 'L0_ffn_W2',
        'L0_ffn_b2', 'L1_gnn_W_proj', 'L1_gnn_b_proj', 'L1_gnn_W_gcn', 'L1_gnn_b_gcn', 'L1_ffn_Wr', 'L1_ffn_br',
        'L1_ffn_W1', 'L1_ffn_b1', 'L1_ffn_W2', 'L1_ffn_b2']


def kernel(**inputs):
    import numpy as np
    import concourse.bacc as bacc
    from concourse.bass_utils import run_bass_kernel_spmd as run

    nc = bacc.Bacc("TRN2", target_bir_lowering=False, num_devices=1)
    arrays, args = {}, []
    for name in _INS:
        a = np.ascontiguousarray(inputs[name])
        arrays[f"in_{name}"] = a
        args.append(nc.dram_tensor(f"in_{name}", a.shape, mybir.dt.from_np(a.dtype), kind="ExternalInput").ap())
    args.append(nc.dram_tensor("out_0", (N, D), mybir.dt.float32, kind="ExternalOutput").ap())
    program(nc, *args)
    r = run(nc, [arrays], core_ids=[0])
    return r.results[0]["out_0"]
```
